# Optimizing a Trainium2 kernel written in Bass

```python
import numpy as np
import jax
import jax.numpy as jnp

def _softmax(x, axis=-1):
    return jax.nn.softmax(x, axis=axis)

def _gelu(x):
    return jax.nn.gelu(x, approximate=True)

def _silu(x):
    return jax.nn.silu(x)

def _sigmoid(x):
    return jax.nn.sigmoid(x)

def _layernorm(x, axis=-1, eps=1e-05):
    m = jnp.mean(x, axis=axis, keepdims=True)
    v = jnp.var(x, axis=axis, keepdims=True)
    return (x - m) / jnp.sqrt(v + eps)

def _scatter_add(tgt, idx, src, axis=0):
    return tgt.at[idx].add(src)

def _segment_sum(src, seg, n):
    return jax.ops.segment_sum(src, seg, n)
kernel_name = 'mk_adaln_ffn_d1_seqx_r8_d6c93b'

def setup_inputs(seed: int=0):
    np.random.seed(seed)
    _w = jnp.asarray

    def _rec_inputs():
        import jax
        import jax.numpy as jnp
        _rk = jax.random.key(seed)
        x = -7.109e-05 + 0.9999 * jax.random.normal(jax.random.fold_in(_rk, 1), (8, 128, 128), jnp.float32)
        _lenS = 128 - jax.random.randint(jax.random.fold_in(_rk, 7), (8,), 0, max(1, 128 // 4) + 1, jnp.int32)
        _lenS2 = 128 - jax.random.randint(jax.random.fold_in(_rk, 8), (8,), 0, max(1, 128 // 4) + 1, jnp.int32)
        itok_B_0_8 = jax.random.randint(jax.random.fold_in(_rk, 11), (8,), 0, 9, jnp.int32)
        return (x, itok_B_0_8)
    x, itok_B_0_8 = _rec_inputs()

    def _L0_cond_setup():
        import jax, jax.numpy as jnp
        import numpy as np
        LN_EPS = 1e-05
        key = jax.random.key(seed)
        ks = jax.random.split(key, 8)
        B, S, H, A, L = (32, 256, 128, 32, 10)
        return {'hidden_states': jax.random.normal(ks[0], (B, S, H), dtype=jnp.float32), 'language_ids': jax.random.randint(ks[1], (B,), 0, L, dtype=jnp.int64), 'W1': jax.random.normal(ks[2], (L, H, A), dtype=jnp.float32) * (1.0 / np.sqrt(H)), 'b1': jnp.zeros((L, A), dtype=jnp.float32), 'W2': jax.random.normal(ks[3], (L, A, H), dtype=jnp.float32) * (1.0 / np.sqrt(A)), 'b2': jnp.zeros((L, H), dtype=jnp.float32), 'gamma': jnp.ones((L, H), dtype=jnp.float32), 'beta': jnp.zeros((L, H), dtype=jnp.float32)}
    _L0_cond_all = _L0_cond_setup()
    _L0_cond_in = {k: v for k, v in _L0_cond_all.items() if k in ('W1', 'b1', 'W2', 'b2', 'gamma', 'beta')}
    del _L0_cond_all

    def _L0_ffn_setup():
        import jax, jax.numpy as jnp
        import numpy as np
        S, B, D, FF, E = (128, 2, 128, 256, 8)
        key = jax.random.key(seed)
        ks = jax.random.split(key, 8)
        s = 0.02
        return {'hidden_states': jax.random.normal(ks[0], (S, B, D), dtype=jnp.float32), 'router_w': jax.random.normal(ks[1], (E, D), dtype=jnp.float32) * s, 'expert_gate': jax.random.normal(ks[2], (E, D, FF), dtype=jnp.float32) * s, 'expert_up': jax.random.normal(ks[3], (E, D, FF), dtype=jnp.float32) * s, 'expert_down': jax.random.normal(ks[4], (E, FF, D), dtype=jnp.float32) * s, 'shared_gate': jax.random.normal(ks[5], (D, FF), dtype=jnp.float32) * s, 'shared_up': jax.random.normal(ks[6], (D, FF), dtype=jnp.float32) * s, 'shared_down': jax.random.normal(ks[7], (FF, D), dtype=jnp.float32) * s}
    _L0_ffn_all = _L0_ffn_setup()
    _L0_ffn_in = {k: v for k, v in _L0_ffn_all.items() if k in ('router_w', 'expert_gate', 'expert_up', 'expert_down', 'shared_gate', 'shared_up', 'shared_down')}
    del _L0_ffn_all
    return {'x': x, 'itok_B_0_8': itok_B_0_8, 'L0_cond_W1': _L0_cond_in['W1'], 'L0_cond_b1': _L0_cond_in['b1'], 'L0_cond_W2': _L0_cond_in['W2'], 'L0_cond_b2': _L0_cond_in['b2'], 'L0_cond_gamma': _L0_cond_in['gamma'], 'L0_cond_beta': _L0_cond_in['beta'], 'L0_ffn_router_w': _L0_ffn_in['router_w'], 'L0_ffn_expert_gate': _L0_ffn_in['expert_gate'], 'L0_ffn_expert_up': _L0_ffn_in['expert_up'], 'L0_ffn_expert_down': _L0_ffn_in['expert_down'], 'L0_ffn_shared_gate': _L0_ffn_in['shared_gate'], 'L0_ffn_shared_up': _L0_ffn_in['shared_up'], 'L0_ffn_shared_down': _L0_ffn_in['shared_down']}

def reference(x, itok_B_0_8, L0_cond_W1, L0_cond_b1, L0_cond_W2, L0_cond_b2, L0_cond_gamma, L0_cond_beta, L0_ffn_router_w, L0_ffn_expert_gate, L0_ffn_expert_up, L0_ffn_expert_down, L0_ffn_shared_gate, L0_ffn_shared_up, L0_ffn_shared_down):
    import jax
    import jax.numpy as jnp

    def _L0_cond_ref(hidden_states, language_ids, W1, b1, W2, b2, gamma, beta):
        import jax, jax.numpy as jnp
        import numpy as np
        LN_EPS = 1e-05
        w1 = W1[language_ids]
        w2 = W2[language_ids]
        h = jnp.einsum('bsh,bha->bsa', hidden_states, w1) + b1[language_ids][:, None, :]
        h = jax.nn.relu(h)
        adapted = jnp.einsum('bsa,bah->bsh', h, w2) + b2[language_ids][:, None, :]
        x = hidden_states + adapted
        mean = jnp.mean(x, axis=-1, keepdims=True)
        var = jnp.mean(jnp.square(x - mean), axis=-1, keepdims=True)
        normed = (x - mean) * jax.lax.rsqrt(var + LN_EPS)
        return normed * gamma[language_ids][:, None, :] + beta[language_ids][:, None, :]

    def _L0_ffn_ref(hidden_states, router_w, expert_gate, expert_up, expert_down, shared_gate, shared_up, shared_down):
        import jax, jax.numpy as jnp
        import numpy as np
        S, B, D, FF, E = (128, 2, 128, 256, 8)
        seq, bs, d = hidden_states.shape
        n_experts = expert_gate.shape[0]
        x = hidden_states.reshape(-1, d)
        logits = jnp.einsum('td,ed->te', x, router_w)
        top_logit = jnp.max(logits, axis=-1)
        top_idx = jnp.argmax(logits, axis=-1)
        score = jax.nn.sigmoid(top_logit)
        onehot = jax.nn.one_hot(top_idx, n_experts, dtype=x.dtype)
        xs = x * score[:, None]
        g = jnp.einsum('td,edf->etf', xs, expert_gate)
        u = jnp.einsum('td,edf->etf', xs, expert_up)
        h = jax.nn.silu(g) * u
        eo = jnp.einsum('etf,efd->etd', h, expert_down)
        moe_out = jnp.einsum('te,etd->td', onehot, eo)
        sh = jax.nn.silu(x @ shared_gate) * (x @ shared_up) @ shared_down
        return (moe_out + sh).reshape(seq, bs, d)
    x = x + _L0_ffn_ref(_L0_cond_ref(x, itok_B_0_8, L0_cond_W1, L0_cond_b1, L0_cond_W2, L0_cond_b2, L0_cond_gamma, L0_cond_beta), L0_ffn_router_w, L0_ffn_expert_gate, L0_ffn_expert_up, L0_ffn_expert_down, L0_ffn_shared_gate, L0_ffn_shared_up, L0_ffn_shared_down)
    return x

_drawn_inputs = setup_inputs


def setup_inputs(seed=0):
    import zlib

    import numpy as np

    out = dict(_drawn_inputs(seed))
    spreads = {'L0_cond_b1': (0.0, 0.8),
     'L0_cond_b2': (0.0, 0.8),
     'L0_cond_gamma': (1.0, 0.6),
     'L0_cond_beta': (0.0, 0.8)}
    factors = {'L0_cond_W1': 8.0,
     'L0_cond_W2': 8.0,
     'L0_ffn_router_w': 8.0,
     'L0_ffn_expert_gate': 8.0,
     'L0_ffn_expert_up': 8.0,
     'L0_ffn_expert_down': 8.0,
     'L0_ffn_shared_gate': 6.311,
     'L0_ffn_shared_up': 6.285,
     'L0_ffn_shared_down': 6.283}
    for name, (base, spread) in spreads.items():
        noise = np.random.default_rng([zlib.crc32(name.encode()), seed]).standard_normal(out[name].shape)
        drawn = base * np.exp(spread * noise) if base else spread * noise
        out[name] = jnp.asarray(drawn.astype(out[name].dtype))
    for name, factor in factors.items():
        out[name] = (out[name] * factor).astype(out[name].dtype)
    return out
```

```python
from contextlib import ExitStack

import concourse.bass as bass
from concourse import mybir
from concourse.alu_op_type import AluOpType as ALU

P = 128
F32 = mybir.dt.float32
BF16 = mybir.dt.bfloat16
I32 = mybir.dt.int32
U32 = mybir.dt.uint32
ACT = mybir.ActivationFunctionType
AX_X = mybir.AxisListType.X

LN_EPS = 1e-5


def adaln_moe_kernel(nc, x, ids, w1, b1, w2, b2, gamma, beta, router_w,
                     expert_gate, expert_up, expert_down, shared_gate, shared_up, shared_down, out):
    B, S, H = x.shape
    L, _, A = w1.shape
    E, _, FF = expert_gate.shape
    K2 = FF // P
    T = B * S
    assert S == P and H == P and K2 == 2
    GROUPS = 2
    GB = B // GROUPS
    OVER = (T - P) // P
    TILES = E + OVER
    ROW = H + 1
    NO_TOKEN = 4 * T

    slots_x = nc.dram_tensor("slots_x", (TILES * P, ROW), F32, kind="Internal").ap()
    slots_r = nc.dram_tensor("slots_r", (TILES * P, H), F32, kind="Internal").ap()
    out_rows = out.rearrange("b s h -> (b s) h")

    with ExitStack() as ctx:
        def sb(name, shape, dt=F32):
            return ctx.enter_context(nc.sbuf_tensor(name, shape, dt))

        def sem(name):
            return ctx.enter_context(nc.semaphore(name))

        bank = [ctx.enter_context(nc.psum_tensor(f"bank{i}", [P, 512], F32)) for i in range(8)]

        ident = sb("ident", [P, P])
        tri = sb("tri", [P, P], BF16)
        ones = sb("ones", [P, P], BF16)
        rev = sb("rev", [P, E])
        before = sb("before", [P, E, E])
        thresholds = sb("thresholds", [P, OVER])
        tile_no = sb("tile_no", [P, OVER])
        lang_no = sb("lang_no", [P, 1])
        empty_row = sb("empty_row", [P, ROW])
        x_tok = sb("x_tok", [P, B, H])
        ids_sb = sb("ids_sb", [L, B], I32)
        w1_all = sb("w1_all", [P, L, A])
        w2_all = sb("w2_all", [A + 1, L, H])
        b1_rows = sb("b1_rows", [L, A])
        gamma_rows = sb("gamma_rows", [L, H])
        beta_rows = sb("beta_rows", [L, H])
        rw_rows = sb("rw_rows", [E, H])
        gu_sh = sb("gu_sh", [P, 2, FF])
        down_sh = sb("down_sh", [P, K2, H])
        gu_ex = sb("gu_ex", [P, E, 2 * FF])
        down_ex = sb("down_ex", [P, E, K2, H])
        lang_hot = sb("lang_hot", [L, B])
        params = sb("params", [P, 3 * B + E])
        w1_sel = sb("w1_sel", [P, B, A])
        xT = sb("xT", [P, B, S])
        hT = sb("hT", [A + 1, B, S])
        v = sb("v", [P, B, H])
        stats = sb("stats", [P, B, 6])
        mv = sb("mv", [P, B, 2])
        std = sb("std", [P, B])
        rstd = sb("rstd", [P, B])
        z = sb("z", [P, B, H])
        nT = sb("nT", [P, B, S])
        top = sb("top", [P, B])
        score = sb("score", [P, B])
        is_top = sb("is_top", [P, B, E])
        ranked = sb("ranked", [P, B, E])
        first = sb("first", [P, B])
        hot = sb("hot", [P, B + 1, E], BF16)
        over_k = sb("over_k", [P, E, OVER])
        over_n = sb("over_n", [P, E])
        over_m = sb("over_m", [P, E, E])
        over_at = sb("over_at", [P, E])
        shift0 = sb("shift0", [P, E])
        shift = sb("shift", [P, E])
        pos1 = sb("pos1", [P, B, E])
        pos2 = sb("pos2", [P, B, E])
        pos3 = sb("pos3", [P, B, E])
        rank = sb("rank", [P, B])
        slot_f = sb("slot_f", [P, B])
        slot = sb("slot", [P, B], U32)
        over_end = sb("over_end", [1, E])
        past = sb("past", [1, OVER, E])
        over_ex_f = sb("over_ex_f", [1, OVER])
        over_ex = sb("over_ex", [1, OVER], I32)
        x_rows = sb("x_rows", [P, B, ROW])
        sg = sb("sg", [P, 2, 512])
        hs = sb("hs", [P, K2, T])
        r_rows = sb("r_rows", [P, B, H])
        slot_x = sb("slot_x", [P, TILES, ROW])
        slot_r = sb("slot_r", [P, TILES, H])
        exT = sb("exT", [P, 2, P])
        eg = sb("eg", [P, 2, FF])
        eh = sb("eh", [P, 2, FF])
        ehT = sb("ehT", [P, 2, K2, P])
        y = sb("y", [P, 4, H])

        x_in = [sem(f"x_in{i}") for i in range(4)]
        ids_in, w1_in, w2_in, par_in = sem("ids_in"), sem("w1_in"), sem("w2_in"), sem("par_in")
        sh_in, gu_in, down_in = sem("sh_in"), sem("gu_in"), sem("down_in")
        pool_const, dve_const = sem("pool_const"), sem("dve_const")
        lang_hot_done, params_ps, params_done = sem("lang_hot_done"), sem("params_ps"), sem("params_done")
        w1_sel_done, xT_ps, xT_done = sem("w1_sel_done"), sem("xT_ps"), sem("xT_done")
        hT_ps, hT_done, ad_ps, v_done = sem("hT_ps"), sem("hT_done"), sem("ad_ps"), sem("v_done")
        stats_done, mv_done, std_done, rstd_done = sem("stats_done"), sem("mv_done"), sem("std_done"), sem("rstd_done")
        z_done, zT_ps, nT_done = sem("z_done"), sem("zT_ps"), sem("nT_done")
        logits_ps, top_done, score_done = sem("logits_ps"), sem("top_done"), sem("score_done")
        route, hot_done, pos_ps, pos_read = sem("route"), sem("hot_done"), sem("pos_ps"), sem("pos_read")
        slot_done, over_ex_done = sem("slot_done"), sem("over_ex_done")
        n_ps, x_rows_done = sem("n_ps"), sem("x_rows_done")
        fill_x, fill_r, x_out, r_out = sem("fill_x"), sem("fill_r"), sem("x_out"), sem("r_out")
        sg_ps, su_ps, sg_done, hs_done = sem("sg_ps"), sem("su_ps"), sem("sg_done"), sem("hs_done")
        sd_ps, r_done = sem("sd_ps"), sem("r_done")
        X_PIECES = [(0, 1), (1, 4), (4, 9), (9, TILES)]
        R_PIECES = [(0, 4), (4, TILES)]
        slot_x_in = [sem(f"slot_x_in{i}") for i in range(len(X_PIECES))]
        slot_r_in = [sem(f"slot_r_in{i}") for i in range(len(R_PIECES))]
        exT_ps, exT_done, gu_ps, eg_done = sem("exT_ps"), sem("exT_done"), sem("gu_ps"), sem("eg_done")
        eh_done, ehT_ps, ehT_done = sem("eh_done"), sem("ehT_ps"), sem("ehT_done")
        y_ps, y_done = sem("y_ps"), sem("y_done")
        y_out = [sem(f"y_out{i}") for i in range(4)]

        def piece_of(pieces, j):
            return next(i for i, (a, b) in enumerate(pieces) if a <= j < b)

        block = ctx.enter_context(nc.Block())

        @block.sync
        def _(sp):
            xr = x.rearrange("b s h -> s b h")
            sp.dma_start(x_tok[:, 0:2, :], xr[:, 0:2, :]).then_inc(x_in[0], 16)
            sp.dma_start(ids_sb[:], ids.rearrange("(a b) -> a b", a=1).to_broadcast([L, B])).then_inc(ids_in, 16)
            sp.dma_start(w1_all[:], w1.rearrange("l h a -> h l a")).then_inc(w1_in, 16)
            sp.dma_start(x_tok[:, 4:6, :], xr[:, 4:6, :]).then_inc(x_in[2], 16)
            sp.dma_start(w2_all[A:A + 1, :, :], b2.rearrange("(a l) h -> a l h", a=1)).then_inc(w2_in, 16)
            sp.dma_start(gamma_rows[:], gamma).then_inc(par_in, 16)
            sp.dma_start(beta_rows[:], beta).then_inc(par_in, 16)
            sp.dma_start(b1_rows[:], b1).then_inc(par_in, 16)
            sp.dma_start(rw_rows[:], router_w).then_inc(par_in, 16)
            sp.wait_ge(dve_const, 2)
            sp.dma_start(slots_x.rearrange("(j p) w -> p j w", p=P),
                         empty_row[:].unsqueeze(1).to_broadcast([P, TILES, ROW])).then_inc(fill_x, 16)
            sp.dma_start(gu_sh[:, 0, :], shared_gate).then_inc(sh_in, 16)
            sp.dma_start(gu_sh[:, 1, :], shared_up).then_inc(sh_in, 16)
            sp.dma_start(down_sh[:], shared_down.rearrange("(k p) h -> p k h", p=P)).then_inc(sh_in, 16)
            sp.dma_start(slots_r.rearrange("(j p) h -> p j h", p=P),
                         empty_row[:, 0:H].unsqueeze(1).to_broadcast([P, TILES, H])).then_inc(fill_r, 16)
            sp.dma_start(gu_ex[:, :, 0:FF], expert_gate.rearrange("e d f -> d e f")).then_inc(gu_in, 16)
            sp.dma_start(gu_ex[:, :, FF:2 * FF], expert_up.rearrange("e d f -> d e f")).then_inc(gu_in, 16)
            sp.dma_start(down_ex[:], expert_down.rearrange("e (k p) h -> p e k h", p=P)).then_inc(down_in, 16)
            sp.wait_ge(x_out, 16 * B)
            for i, (a, b) in enumerate(X_PIECES):
                sp.dma_start(slot_x[:, a:b, :], slots_x[a * P:b * P, :].rearrange("(j p) w -> p j w", p=P)
                             ).then_inc(slot_x_in[i], 16)
            sp.wait_ge(r_out, 16 * B)
            for i, (a, b) in enumerate(R_PIECES):
                sp.dma_start(slot_r[:, a:b, :], slots_r[a * P:b * P, :].rearrange("(j p) h -> p j h", p=P)
                             ).then_inc(slot_r_in[i], 16)

        @block.gpsimd
        def _(pool):
            nc.gpsimd.memset(ident[:], 0.0).then_inc(pool_const, 1)
            pool.wait_ge(pool_const, 1)
            nc.gpsimd.affine_select(out=ident[:], in_=ident[:], compare_op=ALU.not_equal, fill=1.0, base=0,
                                    pattern=[[-1, P]], channel_multiplier=1).then_inc(pool_const, 1)
            nc.gpsimd.iota(lang_no[:], [[0, 1]], base=0, channel_multiplier=1,
                           allow_small_or_imprecise_dtypes=True).then_inc(pool_const, 1)
            pool.wait_ge(ids_in, 16)
            lang = [nc.gpsimd.value_load(ids_sb[0:1, b:b + 1], min_val=0, max_val=L - 1) for b in range(B)]
            pool.wait_ge(w1_in, 16)
            for b in range(B):
                nc.gpsimd.tensor_copy(w1_sel[:, b:b + 1, :], w1_all[:, bass.ds(lang[b], 1), :]).then_inc(w1_sel_done, 1)
            nc.gpsimd.memset(tri[:], 1.0).then_inc(pool_const, 1)
            nc.gpsimd.memset(before[:], 1.0).then_inc(pool_const, 1)
            pool.wait_ge(pool_const, 5)
            nc.gpsimd.affine_select(out=tri[:], in_=tri[:], compare_op=ALU.is_gt, fill=0.0, base=0,
                                    pattern=[[1, P]], channel_multiplier=-1).then_inc(pool_const, 1)
            nc.gpsimd.affine_select(out=before[:], in_=before[:], compare_op=ALU.is_gt, fill=0.0, base=0,
                                    pattern=[[1, E], [-1, E]], channel_multiplier=0).then_inc(pool_const, 1)
            nc.gpsimd.iota(rev[:], [[-1, E]], base=E, channel_multiplier=0,
                           allow_small_or_imprecise_dtypes=True).then_inc(pool_const, 1)
            nc.gpsimd.iota(thresholds[:], [[P, OVER]], base=P, channel_multiplier=0,
                           allow_small_or_imprecise_dtypes=True).then_inc(pool_const, 1)
            nc.gpsimd.iota(tile_no[:], [[1, OVER]], base=0, channel_multiplier=0,
                           allow_small_or_imprecise_dtypes=True).then_inc(pool_const, 1)
            nc.gpsimd.iota(x_rows[:, :, H].bitcast(I32), [[P, B]], base=0, channel_multiplier=1).then_inc(pool_const, 1)
            pool.wait_ge(pool_const, 11)
            pool.wait_ge(fill_x, 16)
            pool.wait_ge(slot_done, 1)
            for b in range(B):
                pool.wait_ge(x_rows_done, b + 1)
                nc.gpsimd.indirect_dma_start(
                    out=slots_x, out_offset=bass.IndirectOffsetOnAxis(ap=slot[:, b:b + 1], axis=0),
                    in_=x_rows[:, b, :], in_offset=None).then_inc(x_out, 16)
            pool.wait_ge(fill_r, 16)
            for b in range(B):
                pool.wait_ge(r_done, b // GB + 1)
                nc.gpsimd.indirect_dma_start(
                    out=slots_r, out_offset=bass.IndirectOffsetOnAxis(ap=slot[:, b:b + 1], axis=0),
                    in_=r_rows[:, b, :], in_offset=None).then_inc(r_out, 16)
            for j in range(TILES):
                pool.wait_ge(slot_x_in[piece_of(X_PIECES, j)], 16)
                pool.wait_ge(y_done, j + 1)
                nc.gpsimd.indirect_dma_start(
                    out=out_rows,
                    out_offset=bass.IndirectOffsetOnAxis(ap=slot_x[:, j, H:H + 1].bitcast(U32), axis=0),
                    in_=y[:, j % 4, :], in_offset=None, bounds_check=T - 1, oob_is_err=False,
                ).then_inc(y_out[j % 4], 16)
            for i in range(4):
                pool.wait_ge(y_out[i], 16 * len(range(i, TILES, 4)))

        @block.tensor
        def _(pe):
            pe.wait_ge(pool_const, 2)
            for g in range(GROUPS):
                for b in range(g * GB, (g + 1) * GB):
                    if b % 2 == 0:
                        pe.wait_ge(x_in[b // 2], 16)
                    last = nc.tensor.transpose(bank[g][:, (b % GB) * S:(b % GB + 1) * S], x_tok[:, b, :], ident[:])
                last.then_inc(xT_ps, 1)
            pe.wait_ge(par_in, 64)
            pe.wait_ge(lang_hot_done, 1)
            nc.tensor.matmul(bank[7][:, 0:B], gamma_rows[:], lang_hot[:], start=True, stop=True)
            nc.tensor.matmul(bank[7][:, B:2 * B], beta_rows[:], lang_hot[:], start=True, stop=True)
            nc.tensor.matmul(bank[7][0:A, 2 * B:3 * B], b1_rows[:], lang_hot[:], start=True, stop=True)
            nc.tensor.transpose(bank[7][:, 3 * B:3 * B + E], rw_rows[:], ident[0:E, 0:E]).then_inc(params_ps, 1)
            for g in range(GROUPS):
                pe.wait_ge(xT_done, g + 1)
                for b in range(g * GB, (g + 1) * GB):
                    pe.wait_ge(w1_sel_done, b + 1)
                    last = nc.tensor.matmul(bank[2 + g][0:A, (b % GB) * S:(b % GB + 1) * S], w1_sel[:, b, :],
                                            xT[:, b, :], start=True, stop=True)
                last.then_inc(hT_ps, 1)
            lang = [nc.tensor.value_load(ids_sb[0:1, b:b + 1], min_val=0, max_val=L - 1) for b in range(B)]
            pe.wait_ge(w2_in, 32)
            pe.wait_ge(dve_const, 1)
            for g in range(GROUPS):
                for b in range(g * GB, (g + 1) * GB):
                    pe.wait_ge(hT_done, b + 1)
                    last = nc.tensor.matmul(bank[4 + g][:, (b % GB) * H:(b % GB + 1) * H], hT[:, b, :],
                                            w2_all[:, bass.ds(lang[b], 1), :], start=True, stop=True)
                last.then_inc(ad_ps, 1)
            pe.wait_ge(params_done, 1)
            for g in range(GROUPS):
                for b in range(g * GB, (g + 1) * GB):
                    pe.wait_ge(z_done, b + 1)
                    last = nc.tensor.transpose(bank[6 + g][:, (b % GB) * S:(b % GB + 1) * S], z[:, b, :], ident[:])
                last.then_inc(zT_ps, 1)
            for b in range(B):
                pe.wait_ge(nT_done, b + 1)
                last = nc.tensor.matmul(bank[0][:, b * E:(b + 1) * E], nT[:, b, :], params[:, 3 * B:3 * B + E],
                                        start=True, stop=True)
            last.then_inc(logits_ps, 1)
            for g in range(GROUPS):
                for b in range(g * GB, (g + 1) * GB):
                    last = nc.tensor.transpose(bank[1 + g][:, (b % GB) * H:(b % GB + 1) * H], nT[:, b, :], ident[:])
                last.then_inc(n_ps, 1)

            def places():
                pe.wait_ge(pool_const, 6)
                pe.wait_ge(dve_const, 4)
                pe.wait_ge(hot_done, 1)
                nc.tensor.matmul(bank[3][:, 0:(B + 1) * E], tri[:], hot[:], start=True, stop=False,
                                 skip_group_check=True)
                for b in range(B):
                    last = nc.tensor.matmul(bank[3][:, (b + 1) * E:(B + 1) * E], ones[:],
                                            hot[:, b:b + 1, :].to_broadcast([P, B - b, E]),
                                            start=False, stop=(b == B - 1), skip_group_check=True)
                last.then_inc(pos_ps, 1)

            pe.wait_ge(sh_in, 48)
            for s in range(GROUPS):
                for k in range(K2):
                    i = s * K2 + k
                    if i >= 2:
                        pe.wait_ge(hs_done, i - 1)
                    nc.tensor.matmul(bank[4 + 2 * k][:], gu_sh[:, 0, k * P:(k + 1) * P],
                                     nT[:, s * GB:(s + 1) * GB, :], start=True, stop=True).then_inc(sg_ps, 1)
                    if i == 0:
                        places()
                    nc.tensor.matmul(bank[5 + 2 * k][:], gu_sh[:, 1, k * P:(k + 1) * P],
                                     nT[:, s * GB:(s + 1) * GB, :], start=True, stop=True).then_inc(su_ps, 1)
            for g in range(GROUPS):
                pe.wait_ge(hs_done, K2 * (g + 1))
                if g == 0:
                    pe.wait_ge(top_done, 1)
                    pe.wait_ge(route, 1)
                pe.wait_ge(x_rows_done, GB * (g + 1) if g == 0 else B)
                for b in range(g * GB, (g + 1) * GB):
                    for k in range(K2):
                        last = nc.tensor.matmul(bank[g][:, (b % GB) * H:(b % GB + 1) * H], hs[:, k, b * S:(b + 1) * S],
                                                down_sh[:, k, :], start=(k == 0), stop=(k == K2 - 1))
                last.then_inc(sd_ps, 1)

            def turn_x(j):
                pe.wait_ge(slot_x_in[piece_of(X_PIECES, j)], 16)
                if j >= 2:
                    pe.wait_ge(exT_done, j - 1)
                nc.tensor.transpose(bank[2 + j % 2][:, 0:P], slot_x[:, j, 0:H], ident[:]).then_inc(exT_ps, 1)

            def gate_up(j, e):
                pe.wait_ge(exT_done, j + 1)
                if j >= 2:
                    pe.wait_ge(eh_done, j - 1)
                nc.tensor.matmul(bank[4 + j % 2][:], exT[:, j % 2, :], gu_ex[:, bass.ds(e, 1), :],
                                 start=True, stop=True).then_inc(gu_ps, 1)

            def turn_h(j):
                pe.wait_ge(eh_done, j + 1)
                if j >= 2:
                    pe.wait_ge(ehT_done, j - 1)
                for k in range(K2):
                    last = nc.tensor.transpose(bank[6 + j % 2][:, k * P:(k + 1) * P], eh[:, j % 2, k * P:(k + 1) * P],
                                               ident[:])
                last.then_inc(ehT_ps, 1)

            def down(j, e):
                pe.wait_ge(ehT_done, j + 1)
                if j >= 2:
                    pe.wait_ge(y_done, j - 1)
                for k in range(K2):
                    last = nc.tensor.matmul(bank[j % 2][:, 0:H], ehT[:, j % 2, k, :], down_ex[:, bass.ds(e, 1), k, :],
                                            start=(k == 0), stop=(k == K2 - 1))
                last.then_inc(y_ps, 1)

            expert = list(range(E))
            pe.wait_ge(over_ex_done, 1)
            expert += [nc.tensor.value_load(over_ex[0:1, i:i + 1], min_val=0, max_val=E - 1) for i in range(OVER)]
            pe.wait_ge(x_rows_done, B)
            pe.wait_ge(pos_read, 1)
            turn_x(0)
            pe.wait_ge(gu_in, 32)
            pe.wait_ge(down_in, 16)
            pe.wait_ge(hs_done, K2 * GROUPS)
            pe.wait_ge(r_done, GROUPS)
            for j in range(TILES + 2):
                if j < TILES:
                    gate_up(j, expert[j])
                if j + 1 < TILES:
                    turn_x(j + 1)
                if 2 <= j:
                    down(j - 2, expert[j - 2])
                if 1 <= j <= TILES:
                    turn_h(j - 1)

        @block.scalar
        def _(act):
            xr = x.rearrange("b s h -> s b h")
            act.dma_start(x_tok[:, 2:4, :], xr[:, 2:4, :]).then_inc(x_in[1], 16)
            act.dma_start(w2_all[0:A, :, :], w2.rearrange("l a h -> a l h")).then_inc(w2_in, 16)
            act.dma_start(x_tok[:, 6:8, :], xr[:, 6:8, :]).then_inc(x_in[3], 16)
            for g in range(GROUPS):
                act.wait_ge(xT_ps, g + 1)
                nc.scalar.activation(xT[:, g * GB:(g + 1) * GB, :], bank[g][:], ACT.Copy).then_inc(xT_done, 1)
            act.wait_ge(params_done, 1)
            for g in range(GROUPS):
                act.wait_ge(hT_ps, g + 1)
                for b in range(g * GB, (g + 1) * GB):
                    nc.scalar.activation(hT[0:A, b, :], bank[2 + g][0:A, (b % GB) * S:(b % GB + 1) * S], ACT.Relu,
                                         bias=params[0:A, 2 * B + b:2 * B + b + 1]).then_inc(hT_done, 1)
            for g in range(GROUPS):
                act.wait_ge(mv_done, (g + 1) * GB)
                nc.scalar.activation(std[:, g * GB:(g + 1) * GB], mv[:, g * GB:(g + 1) * GB, 1], ACT.Sqrt
                                     ).then_inc(std_done, 1)
            for g in range(GROUPS):
                act.wait_ge(zT_ps, g + 1)
                for b in range(g * GB, (g + 1) * GB):
                    nc.scalar.activation(nT[:, b, :], bank[6 + g][:, (b % GB) * S:(b % GB + 1) * S], ACT.Identity,
                                         scale=params[:, b:b + 1], bias=params[:, B + b:B + b + 1]).then_inc(nT_done, 1)
            act.wait_ge(top_done, 1)
            nc.scalar.activation(score[:], top[:], ACT.Sigmoid).then_inc(score_done, 1)
            act.wait_ge(score_done, 1)
            for b in range(B):
                act.wait_ge(n_ps, b // GB + 1)
                nc.scalar.activation(x_rows[:, b, 0:H], bank[1 + b // GB][:, (b % GB) * H:(b % GB + 1) * H], ACT.Copy,
                                     scale=score[:, b:b + 1]).then_inc(x_rows_done, 1)
            for i in range(GROUPS * K2):
                act.wait_ge(sg_ps, i + 1)
                if i >= 2:
                    act.wait_ge(hs_done, i - 1)
                nc.scalar.activation(sg[:, i % 2, :], bank[4 + 2 * (i % K2)][:], ACT.Silu).then_inc(sg_done, 1)

            def x_evacuate(j):
                act.wait_ge(exT_ps, j + 1)
                if j >= 2:
                    act.wait_ge(gu_ps, j - 1)
                nc.scalar.activation(exT[:, j % 2, :], bank[2 + j % 2][:, 0:P], ACT.Copy).then_inc(exT_done, 1)

            x_evacuate(0)
            for j in range(TILES):
                act.wait_ge(gu_ps, j + 1)
                if j >= 2:
                    act.wait_ge(eh_done, j - 1)
                nc.scalar.activation(eg[:, j % 2, :], bank[4 + j % 2][:, 0:FF], ACT.Silu).then_inc(eg_done, 1)
                if j + 1 < TILES:
                    x_evacuate(j + 1)

        @block.vector
        def _(dve):
            nc.vector.memset(hT[A:A + 1, :, :], 1.0).then_inc(dve_const, 1)
            nc.vector.memset(empty_row[:, 0:H], 0.0)
            nc.vector.memset(empty_row[:, H:ROW].bitcast(I32), NO_TOKEN).then_inc(dve_const, 1)
            nc.vector.memset(ones[:], 1.0).then_inc(dve_const, 1)
            nc.vector.memset(hot[:, B, :], 0.0).then_inc(dve_const, 1)
            dve.wait_ge(ids_in, 16)
            dve.wait_ge(pool_const, 3)
            nc.vector.tensor_scalar(lang_hot[:], ids_sb[:], lang_no[0:L, :], None, ALU.is_equal).then_inc(lang_hot_done, 1)
            dve.wait_ge(params_ps, 1)
            nc.vector.tensor_copy(params[:, 0:2 * B], bank[7][:, 0:2 * B])
            nc.vector.tensor_copy(params[0:A, 2 * B:3 * B], bank[7][0:A, 2 * B:3 * B])
            nc.vector.tensor_copy(params[:, 3 * B:3 * B + E], bank[7][:, 3 * B:3 * B + E]).then_inc(params_done, 1)
            for g in range(GROUPS):
                dve.wait_ge(ad_ps, g + 1)
                nc.vector.tensor_tensor(v[:, g * GB:(g + 1) * GB, :], bank[4 + g][:],
                                        x_tok[:, g * GB:(g + 1) * GB, :], ALU.add).then_inc(v_done, 1)
                dve.wait_ge(v_done, g + 1)
                for b in range(g * GB, (g + 1) * GB):
                    nc.vector.bn_stats(stats[:, b, :], v[:, b, :]).then_inc(stats_done, 1)
                for b in range(g * GB, (g + 1) * GB):
                    dve.wait_ge(stats_done, b + 1)
                    nc.vector.bn_aggr(mv[:, b, :], stats[:, b, :]).then_inc(rstd_done, 1)
                dve.wait_ge(rstd_done, GB * (g + 1) + g)
                nc.vector.tensor_scalar(mv[:, g * GB:(g + 1) * GB, 1], mv[:, g * GB:(g + 1) * GB, 1], LN_EPS, None,
                                        ALU.add).then_inc(mv_done, GB)
                dve.wait_ge(std_done, g + 1)
                nc.vector.reciprocal(rstd[:, g * GB:(g + 1) * GB], std[:, g * GB:(g + 1) * GB]).then_inc(rstd_done, 1)
                dve.wait_ge(rstd_done, (GB + 1) * (g + 1))
                for b in range(g * GB, (g + 1) * GB):
                    nc.vector.tensor_scalar(z[:, b, :], v[:, b, :], mv[:, b, 0:1], rstd[:, b:b + 1],
                                            ALU.subtract, ALU.mult).then_inc(z_done, 1)
            dve.wait_ge(logits_ps, 1)
            dve.wait_ge(pool_const, 10)
            logits = bank[0][:, 0:B * E].rearrange("p (b e) -> p b e", b=B)
            nc.vector.tensor_reduce(top[:], logits, AX_X, ALU.max).then_inc(top_done, 1)
            dve.wait_ge(top_done, 1)
            nc.vector.tensor_tensor(is_top[:], logits, top[:].unsqueeze(2).to_broadcast([P, B, E]),
                                    ALU.is_equal).then_inc(route, 1)
            dve.wait_ge(route, 1)
            nc.vector.tensor_tensor(ranked[:], is_top[:], rev[:].unsqueeze(1).to_broadcast([P, B, E]),
                                    ALU.mult).then_inc(route, 1)
            dve.wait_ge(route, 2)
            nc.vector.tensor_reduce(first[:], ranked[:], AX_X, ALU.max).then_inc(route, 1)
            dve.wait_ge(route, 3)
            nc.vector.tensor_tensor(hot[:, 0:B, :], ranked[:], first[:].unsqueeze(2).to_broadcast([P, B, E]),
                                    ALU.is_equal).then_inc(hot_done, 1)
            dve.wait_ge(pos_ps, 1)
            count = bank[3][:, B * E:(B + 1) * E]
            nc.vector.tensor_tensor(over_k[:], count.unsqueeze(2).to_broadcast([P, E, OVER]),
                                    thresholds[:].unsqueeze(1).to_broadcast([P, E, OVER]), ALU.is_gt).then_inc(route, 1)
            dve.wait_ge(route, 4)
            nc.vector.tensor_reduce(over_n[:], over_k[:], AX_X, ALU.add).then_inc(route, 1)
            dve.wait_ge(route, 5)
            nc.vector.tensor_tensor(over_m[:], before[:], over_n[:].unsqueeze(1).to_broadcast([P, E, E]),
                                    ALU.mult).then_inc(route, 1)
            dve.wait_ge(route, 6)
            nc.vector.tensor_reduce(over_at[:], over_m[:], AX_X, ALU.add).then_inc(route, 1)
            dve.wait_ge(route, 7)
            nc.vector.tensor_tensor(shift0[:], over_at[:], rev[:], ALU.add).then_inc(route, 1)
            dve.wait_ge(route, 8)
            nc.vector.tensor_scalar(shift[:], shift0[:], -1.0, float(P), ALU.add, ALU.mult).then_inc(route, 1)
            dve.wait_ge(route, 9)
            place = bank[3][:, 0:B * E].rearrange("p (b e) -> p b e", b=B)
            nc.vector.scalar_tensor_tensor(out=pos1[:], in0=place, scalar=float(P) - 0.5,
                                           in1=shift[:].unsqueeze(1).to_broadcast([P, B, E]),
                                           op0=ALU.is_gt, op1=ALU.mult).then_inc(route, 1)
            dve.wait_ge(route, 10)
            nc.vector.tensor_tensor(pos2[:], pos1[:], place, ALU.add).then_inc(pos_read, 1)
            dve.wait_ge(pos_read, 1)
            nc.vector.tensor_tensor(pos3[:], pos2[:], hot[:, 0:B, :], ALU.mult).then_inc(route, 1)
            dve.wait_ge(route, 11)
            nc.vector.tensor_reduce(rank[:], pos3[:], AX_X, ALU.add).then_inc(route, 1)
            dve.wait_ge(route, 12)
            nc.vector.scalar_tensor_tensor(out=slot_f[:], in0=first[:], scalar=-float(P), in1=rank[:],
                                           op0=ALU.mult, op1=ALU.add).then_inc(route, 1)
            dve.wait_ge(route, 13)
            nc.vector.tensor_scalar(slot[:], slot_f[:], float(P * E), None, ALU.add).then_inc(slot_done, 1)
            nc.vector.tensor_tensor(over_end[:], over_at[0:1, :], over_n[0:1, :], ALU.add).then_inc(route, 1)
            dve.wait_ge(route, 14)
            nc.vector.tensor_tensor(past[:], tile_no[0:1, :].unsqueeze(2).to_broadcast([1, OVER, E]),
                                    over_end[:].unsqueeze(1).to_broadcast([1, OVER, E]), ALU.is_ge).then_inc(route, 1)
            dve.wait_ge(route, 15)
            nc.vector.tensor_reduce(over_ex_f[:], past[:], AX_X, ALU.add).then_inc(route, 1)
            dve.wait_ge(route, 16)
            nc.vector.tensor_scalar(over_ex[:], over_ex_f[:], float(E - 1), None, ALU.min).then_inc(over_ex_done, 1)
            for i in range(GROUPS * K2):
                s, k = i // K2, i % K2
                dve.wait_ge(sg_done, i + 1)
                dve.wait_ge(su_ps, i + 1)
                nc.vector.tensor_tensor(hs[:, k, s * 512:(s + 1) * 512], sg[:, i % 2, :], bank[5 + 2 * k][:],
                                        ALU.mult).then_inc(hs_done, 1)
            for g in range(GROUPS):
                dve.wait_ge(sd_ps, g + 1)
                nc.vector.tensor_tensor(r_rows[:, g * GB:(g + 1) * GB, :], bank[g][:],
                                        x_tok[:, g * GB:(g + 1) * GB, :], ALU.add).then_inc(r_done, 1)

            def gated(j):
                dve.wait_ge(eg_done, j + 1)
                if j >= 2:
                    dve.wait_ge(ehT_ps, j - 1)
                nc.vector.tensor_tensor(eh[:, j % 2, :], eg[:, j % 2, :], bank[4 + j % 2][:, FF:2 * FF],
                                        ALU.mult).then_inc(eh_done, 1)

            def finish(j):
                dve.wait_ge(y_ps, j + 1)
                dve.wait_ge(slot_r_in[piece_of(R_PIECES, j)], 16)
                if j >= 4:
                    dve.wait_ge(y_out[j % 4], 16 * (j // 4))
                nc.vector.tensor_tensor(y[:, j % 4, :], bank[j % 2][:, 0:H], slot_r[:, j, :],
                                        ALU.add).then_inc(y_done, 1)

            def h_evacuate(j):
                dve.wait_ge(ehT_ps, j + 1)
                if j >= 2:
                    dve.wait_ge(y_ps, j - 1)
                nc.vector.tensor_copy(ehT[:, j % 2, :, :], bank[6 + j % 2][:, 0:FF]).then_inc(ehT_done, 1)

            for j in range(1, TILES + 3):
                if j <= TILES:
                    gated(j - 1)
                if 2 <= j < TILES + 2:
                    finish(j - 2)
                if j <= TILES:
                    h_evacuate(j - 1)


_INS = ["x", "itok_B_0_8", "L0_cond_W1", "L0_cond_b1", "L0_cond_W2", "L0_cond_b2", "L0_cond_gamma", "L0_cond_beta",
        "L0_ffn_router_w", "L0_ffn_expert_gate", "L0_ffn_expert_up", "L0_ffn_expert_down",
        "L0_ffn_shared_gate", "L0_ffn_shared_up", "L0_ffn_shared_down"]


def kernel(**inputs):
    import numpy as _np
    import concourse.bacc as _bacc
    from concourse import mybir as _mybir
    from concourse.bass_utils import run_bass_kernel_spmd as _run

    nc = _bacc.Bacc("TRN2", target_bir_lowering=False, num_devices=1)
    arrays, args = {}, []
    for name in _INS:
        a = _np.ascontiguousarray(inputs[name])
        arrays[f"in_{name}_dram"] = a
        args.append(nc.dram_tensor(f"in_{name}_dram", a.shape, _mybir.dt.from_np(a.dtype), kind="ExternalInput").ap())
    out = nc.dram_tensor("out_dram", inputs["x"].shape, _mybir.dt.float32, kind="ExternalOutput").ap()
    adaln_moe_kernel(nc, *args, out)
    r = _run(nc, [arrays], core_ids=[0])
    return r.results[0]["out_dram"]
```

```python
from contextlib import ExitStack

import concourse.bass as bass
from concourse import mybir
from concourse.alu_op_type import AluOpType as ALU

P = 128
F32 = mybir.dt.float32
BF16 = mybir.dt.bfloat16
I32 = mybir.dt.int32
U32 = mybir.dt.uint32
ACT = mybir.ActivationFunctionType
AX_X = mybir.AxisListType.X

LN_EPS = 1e-5


def adaln_moe_kernel(nc, x, ids, w1, b1, w2, b2, gamma, beta, router_w,
                     expert_gate, expert_up, expert_down, shared_gate, shared_up, shared_down, out):
    B, S, H = x.shape
    L, _, A = w1.shape
    E, _, FF = expert_gate.shape
    K2 = FF // P
    T = B * S
    assert S == P and H == P and K2 == 2
    GROUPS = 2
    GB = B // GROUPS
    OVER = (T - P) // P
    TILES = E + OVER
    RARE = 4
    COUNT = 2 * E
    ROW = H + 1
    SEGMENTS = [(0, 4), (4, B)]
    NO_TOKEN = 4 * T

    slots_x = nc.dram_tensor("slots_x", (TILES * P, ROW), F32, kind="Internal").ap()
    slots_r = nc.dram_tensor("slots_r", (TILES * P, H), F32, kind="Internal").ap()
    out_rows = out.rearrange("b s h -> (b s) h")

    with ExitStack() as ctx:
        def sb(name, shape, dt=F32):
            return ctx.enter_context(nc.sbuf_tensor(name, shape, dt))

        def sem(name):
            return ctx.enter_context(nc.semaphore(name))

        bank = [ctx.enter_context(nc.psum_tensor(f"bank{i}", [P, 512], F32)) for i in range(8)]

        ident = sb("ident", [P, P])
        tri = sb("tri", [P, P], BF16)
        ones = sb("ones", [P, P], BF16)
        rev = sb("rev", [P, E])
        before = sb("before", [E, E + 1], BF16)
        behind = sb("behind", [1, E + 1], BF16)
        thresholds = sb("thresholds", [E, OVER])
        bounds = sb("bounds", [1, OVER, E - 1])
        warm = sb("warm", [P, P], BF16)
        lang_no = sb("lang_no", [P, 1])
        empty_row = sb("empty_row", [P, ROW])
        x_tok = sb("x_tok", [P, B, H])
        ids_sb = sb("ids_sb", [L, B], I32)
        w1_all = sb("w1_all", [P, L, A])
        w2_all = sb("w2_all", [A + 1, L, H])
        b1_rows = sb("b1_rows", [L, A])
        gamma_rows = sb("gamma_rows", [L, H])
        beta_rows = sb("beta_rows", [L, H])
        rw_rows = sb("rw_rows", [E, H])
        gu_sh = sb("gu_sh", [P, 2, FF])
        down_sh = sb("down_sh", [P, K2, H])
        gu_ex = sb("gu_ex", [P, E, 2 * FF])
        down_ex = sb("down_ex", [P, E, K2, H])
        lang_hot = sb("lang_hot", [L, B])
        params = sb("params", [P, 3 * B + E])
        w1_sel = sb("w1_sel", [P, B, A])
        xT = sb("xT", [P, B, S])
        hT = sb("hT", [A + 1, B, S])
        stats = sb("stats", [P, B, 6])
        mv = sb("mv", [P, B, 2])
        std = sb("std", [P, B])
        eps = sb("eps", [P, 1])
        rstd = sb("rstd", [P, B])
        z = sb("z", [P, B, H])
        nT = sb("nT", [P, B, S])
        top = sb("top", [P, B])
        half_tanh = sb("half_tanh", [P, B])
        score = sb("score", [P, B])
        is_top = sb("is_top", [P, B, E])
        ranked = sb("ranked", [P, B, E])
        first = sb("first", [P, B])
        hot = sb("hot", [P, B, E], BF16)
        over_k = sb("over_k", [E, OVER])
        over_n = sb("over_n", [E, 1], BF16)
        base = sb("base", [P, B])
        place_hot = sb("place_hot", [P, B, E])
        place = sb("place", [P, B])
        slot_fix = sb("slot_fix", [P, B])
        shift_hot = sb("shift_hot", [P, B, E])
        shift = sb("shift", [P, B])
        shifted = sb("shifted", [P, B])
        slot = sb("slot", [P, B], U32)
        past = sb("past", [1, OVER, E - 1])
        over_ex_f = sb("over_ex_f", [1, OVER])
        over_size = sb("over_size", [1, 1], I32)
        over_ex = sb("over_ex", [1, OVER], I32)
        x_rows = sb("x_rows", [P, B, ROW])
        sg = sb("sg", [P, 2, 512])
        hs = sb("hs", [P, K2, T])
        r_rows = sb("r_rows", [P, B, H])
        slot_x = sb("slot_x", [P, TILES, ROW])
        slot_r = sb("slot_r", [P, TILES, H])
        exT = sb("exT", [P, 2, P])
        eg = sb("eg", [P, 2, FF])
        eh = sb("eh", [P, 3, FF])
        ehT = sb("ehT", [P, 2, K2, P])
        y = sb("y", [P, TILES, H])

        x_in = [sem(f"x_in{i}") for i in range(2)]
        ids_in, b1_in, w1_in, w2_in, par_in = sem("ids_in"), sem("b1_in"), sem("w1_in"), sem("w2_in"), sem("par_in")
        sh_in, gu_in, down_in = sem("sh_in"), sem("gu_in"), sem("down_in")
        pool_const, dve_const = sem("pool_const"), sem("dve_const")
        lang_hot_done, params_ps, params_done = sem("lang_hot_done"), sem("params_ps"), sem("params_done")
        w1_even, w1_odd, xT_ps, xT_done = sem("w1_even"), sem("w1_odd"), sem("xT_ps"), sem("xT_done")
        hT_ps, hT_even, hT_odd, v_ps = sem("hT_ps"), sem("hT_even"), sem("hT_odd"), sem("v_ps")
        stats_done, mv_done, std_done, rstd_done = sem("stats_done"), sem("mv_done"), sem("std_done"), sem("rstd_done")
        z_done, zT_ps = sem("z_done"), sem("zT_ps")
        nT_act, nT_dve = sem("nT_act"), sem("nT_dve")
        logits_ps, top_done, tanh_done, score_done = sem("logits_ps"), sem("top_done"), sem("tanh_done"), sem("score_done")
        route, hot_done, pos_ps, pos_read = sem("route"), sem("hot_done"), sem("pos_ps"), sem("pos_read")
        count_ps, over_n_done, shift_ps, warm_set = sem("count_ps"), sem("over_n_done"), sem("shift_ps"), sem("warm_set")
        slot_done, over_ex_done = sem("slot_done"), sem("over_ex_done")
        n_ps, scaled = sem("n_ps"), sem("scaled")
        fill_x, fill_r, x_out, r_out = sem("fill_x"), sem("fill_r"), sem("x_out"), sem("r_out")
        sg_ps, su_ps, sg_done, hs_done = sem("sg_ps"), sem("su_ps"), sem("sg_done"), sem("hs_done")
        sd_ps, r_done = sem("sd_ps"), sem("r_done")
        PIECES = [(E, E + 1), (E + 1, E + RARE), (0, 3), (3, E), (E + RARE, TILES)]
        slot_x_in = [sem(f"slot_x_in{i}") for i in range(len(PIECES))]
        slot_r_in = [sem(f"slot_r_in{i}") for i in range(len(PIECES))]

        class Run:
            def __init__(self, name, tiles, lag):
                self.lag = lag
                self.tiles = tiles
                self.n = len(tiles)
                self.over = sum(t >= E for t in tiles)
                self.exT_ps, self.exT_done = sem(f"{name}_exT_ps"), sem(f"{name}_exT_done")
                self.gu_ps, self.eg_done, self.eh_done = sem(f"{name}_gu_ps"), sem(f"{name}_eg_done"), sem(f"{name}_eh_done")
                self.ehT_ps, self.ehT_done = sem(f"{name}_ehT_ps"), sem(f"{name}_ehT_done")
                self.y_ps, self.y_copied = sem(f"{name}_y_ps"), sem(f"{name}_y_copied")
                self.y_done, self.y_out = sem(f"{name}_y_done"), sem(f"{name}_y_out")

        rare = Run("rare", list(range(E + RARE, TILES)), lag=2)
        main = Run("main", list(range(E, E + RARE)) + list(range(E)), lag=4)

        def rare_in_use(engine):
            engine.wait_ge(over_ex_done, 2)
            return engine.value_load(over_size[0:1, 0:1], min_val=-P, max_val=P * (OVER - 1)) > P * (RARE - 1)

        def piece_of(j):
            return next(i for i, (a, b) in enumerate(PIECES) if a <= j < b)

        EX_X, EX_GU, EX_H, EX_Y = (2, 5), (0, 1), (4, 7), (3, 6)
        SH_BANKS = [(4, 7), (0, 1)]

        def h_place(b):
            bk = bank[(2, 3, 6, 7)[2 * (b // GB) + b % 2]]
            at = (b % GB) // 2
            return bk[0:A, at * S:(at + 1) * S]

        def load_numbers(engine, row, n, high):
            values = []
            for i in range(0, n, 4):
                regs = [engine.alloc_register(f"{row.name}_{k}") for k in range(i, min(i + 4, n))]
                engine.reg_load(regs, row[0:1, i:i + len(regs)])
                values += [engine.snap(r, min_val=0, max_val=high) for r in regs]
            return values

        block = ctx.enter_context(nc.Block())

        @block.sync
        def _(sp):
            xr = x.rearrange("b s h -> s b h")
            sp.dma_start(x_tok[:, 0:GB, :], xr[:, 0:GB, :]).then_inc(x_in[0], 16)
            sp.dma_start(ids_sb[:], ids.rearrange("(a b) -> a b", a=1).to_broadcast([L, B])).then_inc(ids_in, 16)
            sp.dma_start(x_tok[:, GB:B, :], xr[:, GB:B, :]).then_inc(x_in[1], 16)
            sp.dma_start(b1_rows[:], b1).then_inc(b1_in, 16)
            sp.dma_start(w2_all[0:A, :, :], w2.rearrange("l a h -> a l h")).then_inc(w2_in, 16)
            sp.dma_start(w2_all[A:A + 1, :, :], b2.rearrange("(a l) h -> a l h", a=1)).then_inc(w2_in, 16)
            sp.dma_start(gamma_rows[:], gamma).then_inc(par_in, 16)
            sp.dma_start(beta_rows[:], beta).then_inc(par_in, 16)
            sp.dma_start(rw_rows[:], router_w).then_inc(par_in, 16)
            sp.dma_start(gu_sh[:, 0, :], shared_gate).then_inc(sh_in, 16)
            sp.dma_start(gu_sh[:, 1, :], shared_up).then_inc(sh_in, 16)
            sp.dma_start(down_sh[:], shared_down.rearrange("(k p) h -> p k h", p=P)).then_inc(sh_in, 16)
            sp.wait_ge(dve_const, 3)
            sp.dma_start(slots_x.rearrange("(j p) w -> p j w", p=P),
                         empty_row[:].unsqueeze(1).to_broadcast([P, TILES, ROW])).then_inc(fill_x, 16)
            sp.dma_start(slots_r.rearrange("(j p) h -> p j h", p=P),
                         empty_row[:, 0:H].unsqueeze(1).to_broadcast([P, TILES, H])).then_inc(fill_r, 16)
            sp.dma_start(gu_ex[:, :, 0:FF], expert_gate.rearrange("e d f -> d e f")).then_inc(gu_in, 16)
            sp.dma_start(gu_ex[:, :, FF:2 * FF], expert_up.rearrange("e d f -> d e f")).then_inc(gu_in, 16)
            sp.dma_start(down_ex[:], expert_down.rearrange("e (k p) h -> p e k h", p=P)).then_inc(down_in, 16)
            sp.wait_ge(x_out, 16 * B)
            for i, (a, b) in enumerate(PIECES):
                sp.dma_start(slot_x[:, a:b, :], slots_x[a * P:b * P, :].rearrange("(j p) w -> p j w", p=P)
                             ).then_inc(slot_x_in[i], 16)
            sp.wait_ge(r_out, 16 * B)
            for i, (a, b) in enumerate(PIECES):
                sp.dma_start(slot_r[:, a:b, :], slots_r[a * P:b * P, :].rearrange("(j p) h -> p j h", p=P)
                             ).then_inc(slot_r_in[i], 16)

        @block.gpsimd
        def _(pool):
            nc.gpsimd.memset(ident[:], 0.0).then_inc(pool_const, 1)
            pool.wait_ge(pool_const, 1)
            nc.gpsimd.affine_select(out=ident[:], in_=ident[:], compare_op=ALU.not_equal, fill=1.0, base=0,
                                    pattern=[[-1, P]], channel_multiplier=1).then_inc(pool_const, 1)
            nc.gpsimd.iota(lang_no[:], [[0, 1]], base=0, channel_multiplier=1,
                           allow_small_or_imprecise_dtypes=True).then_inc(pool_const, 1)
            pool.wait_ge(ids_in, 16)
            lang = load_numbers(nc.gpsimd, ids_sb, B, L - 1)
            pool.wait_ge(w1_in, 16)
            for b in range(0, B, 2):
                nc.gpsimd.tensor_copy(w1_sel[:, b:b + 1, :], w1_all[:, bass.ds(lang[b], 1), :]).then_inc(w1_even, 1)
            nc.gpsimd.memset(tri[:], 1.0).then_inc(pool_const, 1)
            nc.gpsimd.memset(before[:], float(P)).then_inc(pool_const, 1)
            pool.wait_ge(pool_const, 5)
            nc.gpsimd.affine_select(out=tri[:], in_=tri[:], compare_op=ALU.is_gt, fill=0.0, base=0,
                                    pattern=[[1, P]], channel_multiplier=-1).then_inc(pool_const, 1)
            nc.gpsimd.affine_select(out=before[:], in_=before[:], compare_op=ALU.is_gt, fill=0.0, base=0,
                                    pattern=[[1, E + 1]], channel_multiplier=-1).then_inc(pool_const, 1)
            nc.gpsimd.iota(rev[:], [[-1, E]], base=E, channel_multiplier=0,
                           allow_small_or_imprecise_dtypes=True).then_inc(pool_const, 1)
            nc.gpsimd.iota(behind[:], [[-P, E + 1]], base=P * (E - 1), channel_multiplier=0,
                           allow_small_or_imprecise_dtypes=True).then_inc(pool_const, 1)
            nc.gpsimd.iota(thresholds[:], [[P, OVER]], base=P, channel_multiplier=0,
                           allow_small_or_imprecise_dtypes=True).then_inc(pool_const, 1)
            nc.gpsimd.iota(bounds[:], [[P, OVER], [-P, E - 1]], base=P * (E - 2), channel_multiplier=0,
                           allow_small_or_imprecise_dtypes=True).then_inc(pool_const, 1)
            nc.gpsimd.iota(x_rows[:, :, H].bitcast(I32), [[P, B]], base=0, channel_multiplier=1).then_inc(pool_const, 1)
            pool.wait_ge(pool_const, 12)
            pool.wait_ge(fill_x, 16)
            pool.wait_ge(slot_done, 1)
            for b in range(B):
                pool.wait_ge(scaled, b + 1)
                nc.gpsimd.indirect_dma_start(
                    out=slots_x, out_offset=bass.IndirectOffsetOnAxis(ap=slot[:, b:b + 1], axis=0),
                    in_=x_rows[:, b, :], in_offset=None).then_inc(x_out, 16)
            pool.wait_ge(fill_r, 16)
            for b in range(B):
                pool.wait_ge(r_done, b + 1)
                nc.gpsimd.indirect_dma_start(
                    out=slots_r, out_offset=bass.IndirectOffsetOnAxis(ap=slot[:, b:b + 1], axis=0),
                    in_=r_rows[:, b, :], in_offset=None).then_inc(r_out, 16)
            def tiles_out(run):
                for i, tile in enumerate(run.tiles):
                    pool.wait_ge(slot_x_in[piece_of(tile)], 16)
                    pool.wait_ge(run.y_done, i + 1)
                    nc.gpsimd.indirect_dma_start(
                        out=out_rows,
                        out_offset=bass.IndirectOffsetOnAxis(ap=slot_x[:, tile, H:H + 1].bitcast(U32), axis=0),
                        in_=y[:, tile, :], in_offset=None, bounds_check=T - 1, oob_is_err=False,
                    ).then_inc(run.y_out, 16)
                pool.wait_ge(run.y_out, 16 * run.n)

            with nc.gpsimd.If(rare_in_use(nc.gpsimd)):
                tiles_out(rare)
            tiles_out(main)
            pool.wait_ge(slot_x_in[-1], 16)
            pool.wait_ge(slot_r_in[-1], 16)

        @block.tensor
        def _(pe):
            def keep_warm(n, blocks=4):
                for _ in range(n):
                    nc.tensor.matmul(bank[7][:, 0:blocks * P], warm[:], warm[:].unsqueeze(1).to_broadcast([P, blocks, P]),
                                     start=True, stop=True)

            pe.wait_ge(warm_set, 1)
            keep_warm(8)
            pe.wait_ge(pool_const, 2)
            for g in range(GROUPS):
                pe.wait_ge(x_in[g], 16)
                for b in range(g * GB, (g + 1) * GB):
                    last = nc.tensor.transpose(bank[g][:, (b % GB) * S:(b % GB + 1) * S], x_tok[:, b, :], ident[:])
                last.then_inc(xT_ps, 1)
            lang = load_numbers(nc.tensor, ids_sb, B, L - 1)
            for g in range(GROUPS):
                pe.wait_ge(xT_done, g + 1)
                for b in [*range(g * GB, (g + 1) * GB, 2), *range(g * GB + 1, (g + 1) * GB, 2)]:
                    pe.wait_ge(w1_odd if b % 2 else w1_even, b // 2 + 1)
                    last = nc.tensor.matmul(h_place(b), w1_sel[:, b, :], xT[:, b, :], start=True, stop=True)
                    if b % GB >= GB - 2:
                        last.then_inc(hT_ps, 1)
                if g == 0:
                    pe.wait_ge(b1_in, 16)
                    pe.wait_ge(lang_hot_done, 1)
                    nc.tensor.matmul(bank[0][0:A, 2 * B:3 * B], b1_rows[:], lang_hot[:], start=True, stop=True
                                     ).then_inc(params_ps, 1)
            pe.wait_ge(w2_in, 32)
            pe.wait_ge(dve_const, 1)
            for g in range(GROUPS):
                for b in range(g * GB, (g + 1) * GB):
                    nc.tensor.matmul(bank[4 + g][:, (b % GB) * H:(b % GB + 1) * H], xT[:, b, :], ident[:],
                                     start=(b % GB == 0), stop=False, skip_group_check=True)
                for b in range(g * GB, (g + 1) * GB):
                    pe.wait_ge(hT_odd if b % 2 else hT_even, b // 2 + 1)
                    last = nc.tensor.matmul(bank[4 + g][:, (b % GB) * H:(b % GB + 1) * H], hT[:, b, :],
                                            w2_all[:, bass.ds(lang[b], 1), :], start=False, stop=(b % GB == GB - 1),
                                            skip_group_check=True)
                last.then_inc(v_ps, 1)
            pe.wait_ge(par_in, 48)
            pe.wait_ge(params_done, 1)
            nc.tensor.matmul(bank[1][:, 0:B], gamma_rows[:], lang_hot[:], start=True, stop=True)
            nc.tensor.matmul(bank[1][:, B:2 * B], beta_rows[:], lang_hot[:], start=True, stop=True)
            nc.tensor.transpose(bank[1][:, 3 * B:3 * B + E], rw_rows[:], ident[0:E, 0:E]).then_inc(params_ps, 1)
            keep_warm(8)

            def turn_z(b, at):
                pe.wait_ge(z_done, b + 1)
                return nc.tensor.transpose(at, z[:, b, :], ident[:])

            def router(g):
                for b in range(g * GB, (g + 1) * GB):
                    if b in (4, 5):
                        pe.wait_ge(nT_dve, b - 3)
                    else:
                        pe.wait_ge(nT_act, b + 1 if b < 4 else b - 1)
                    last = nc.tensor.matmul(bank[2][:, b * E:(b + 1) * E], nT[:, b, :], params[:, 3 * B:3 * B + E],
                                            start=True, stop=True)
                return last

            def shared_up(i, u):
                (a, b), k = SEGMENTS[i // K2], i % K2
                if i >= 2:
                    pe.wait_ge(hs_done, i - 1)
                nc.tensor.matmul(bank[SH_BANKS[k][u]][:, 0:(b - a) * S], gu_sh[:, u, k * P:(k + 1) * P],
                                 nT[:, a:b, :], start=True, stop=True).then_inc(su_ps if u else sg_ps, 1)

            def shared_down(s):
                pe.wait_ge(hs_done, K2 * (s + 1))
                pe.wait_ge(scaled, GB)
                pe.wait_ge(pos_read, 1)
                for b in range(*SEGMENTS[s]):
                    if b >= 2:
                        pe.wait_ge(r_done, b - 1)
                    for k in range(K2):
                        last = nc.tensor.matmul(bank[(3, 2)[b % 2]][:, 0:H], hs[:, k, b * S:(b + 1) * S],
                                                down_sh[:, k, :], start=(k == 0), stop=(k == K2 - 1))
                    last.then_inc(sd_ps, 1)

            for b in range(GB):
                keep_warm(1, 2)
                last = turn_z(b, bank[0][:, b * S:(b + 1) * S])
            last.then_inc(zT_ps, 1)
            pe.wait_ge(params_done, 2)
            for b in (4, 5):
                keep_warm(1, 2)
                last = turn_z(b, bank[1][:, (b - 4) * S:(b - 3) * S])
            last.then_inc(zT_ps, 1)
            for b in (6, 7):
                keep_warm(1, 2)
                last = turn_z(b, bank[6][:, (b - 6) * S:(b - 5) * S])
            last.then_inc(zT_ps, 1)
            keep_warm(1)
            router(0)
            keep_warm(1)
            router(1).then_inc(logits_ps, 1)

            def turn_n(g):
                for b in range(g * GB, (g + 1) * GB):
                    last = nc.tensor.transpose(bank[3 + 3 * g][:, (b % GB) * H:(b % GB + 1) * H], nT[:, b, :], ident[:])
                last.then_inc(n_ps, 1)

            turn_n(0)
            pe.wait_ge(sh_in, 48)
            shared_up(0, 0)

            pe.wait_ge(pool_const, 12)
            pe.wait_ge(dve_const, 4)
            pe.wait_ge(hot_done, 1)
            for b in range(B):
                last = nc.tensor.matmul(bank[5][0:E, COUNT:COUNT + 1], hot[:, b, :], ones[:, 0:1], start=(b == 0), stop=(b == B - 1))
            last.then_inc(count_ps, 1)
            nc.tensor.matmul(bank[2][:, 0:B * E], tri[:], hot[:], start=True, stop=False, skip_group_check=True)
            for b in range(B - 1):
                last = nc.tensor.matmul(bank[2][:, (b + 1) * E:B * E], ones[:],
                                        hot[:, b:b + 1, :].to_broadcast([P, B - 1 - b, E]),
                                        start=False, stop=(b == B - 2), skip_group_check=True)
            last.then_inc(pos_ps, 1)
            turn_n(1)
            pe.wait_ge(over_n_done, 1)
            nc.tensor.matmul(bank[5][:, 0:E + 1], ones[0:1, :], behind[:], start=True, stop=False)
            nc.tensor.matmul(bank[5][:, 0:E + 1], over_n[:].to_broadcast([E, P]), before[:],
                             start=False, stop=True).then_inc(shift_ps, 1)
            shared_up(0, 1)
            shared_up(1, 0)
            shared_up(1, 1)
            for s in range(len(SEGMENTS)):
                if s + 1 < len(SEGMENTS):
                    shared_up(K2 * (s + 1), 0)
                    shared_up(K2 * (s + 1), 1)
                shared_down(s)
                if s + 1 < len(SEGMENTS):
                    shared_up(K2 * (s + 1) + 1, 0)
                    shared_up(K2 * (s + 1) + 1, 1)

            def expert_tiles(run, expert):
                def turn_x(i):
                    pe.wait_ge(slot_x_in[piece_of(run.tiles[i])], 16)
                    if i >= 2:
                        pe.wait_ge(run.exT_done, i - 1)
                    nc.tensor.transpose(bank[EX_X[i % 2]][:, 0:P], slot_x[:, run.tiles[i], 0:H], ident[:]
                                        ).then_inc(run.exT_ps, 1)

                def gate_up(i):
                    pe.wait_ge(run.exT_done, i + 1)
                    if i >= 2:
                        pe.wait_ge(run.eh_done, i - 1)
                    if i < run.over:
                        last = nc.tensor.matmul(bank[EX_GU[i % 2]][:], exT[:, i % 2, :],
                                                gu_ex[:, bass.ds(expert[i], 1), :], start=True, stop=True)
                    else:
                        for k in range(2 * K2):
                            last = nc.tensor.matmul(bank[EX_GU[i % 2]][:, k * P:(k + 1) * P],
                                                    gu_ex[:, expert[i], k * P:(k + 1) * P], exT[:, i % 2, :],
                                                    start=True, stop=True)
                    last.then_inc(run.gu_ps, 1)

                def turn_h(i):
                    pe.wait_ge(run.eh_done, i + 1)
                    if i >= 2:
                        pe.wait_ge(run.ehT_done, i - 1)
                    for k in range(K2):
                        last = nc.tensor.transpose(bank[EX_H[i % 2]][:, k * P:(k + 1) * P],
                                                   eh[:, i % 3, k * P:(k + 1) * P], ident[:])
                    last.then_inc(run.ehT_ps, 1)

                def down(i):
                    if i < run.over:
                        pe.wait_ge(run.ehT_done, i + 1)
                    else:
                        pe.wait_ge(run.eh_done, i + 1)
                    if i >= 2:
                        pe.wait_ge(run.y_copied, i - 1)
                    for k in range(K2):
                        hidden = ehT[:, i % 2, k, :] if i < run.over else eh[:, i % 3, k * P:(k + 1) * P]
                        last = nc.tensor.matmul(bank[EX_Y[i % 2]][:, 0:H], hidden,
                                                down_ex[:, bass.ds(expert[i], 1), k, :],
                                                start=(k == 0), stop=(k == K2 - 1))
                    last.then_inc(run.y_ps, 1)

                turn_x(0)
                for i in range(run.n + 2):
                    if i + 1 < run.n:
                        turn_x(i + 1)
                    if i - 2 >= run.over:
                        down(i - 2)
                    if i < run.n:
                        gate_up(i)
                    if 0 <= i - 2 < run.over:
                        down(i - 2)
                    if 1 <= i <= run.over:
                        turn_h(i - 1)

            pe.wait_ge(over_ex_done, 1)
            expert = load_numbers(nc.tensor, over_ex, OVER, E - 1)
            pe.wait_ge(r_done, B)
            pe.wait_ge(gu_in, 32)
            pe.wait_ge(down_in, 16)
            with nc.tensor.If(rare_in_use(nc.tensor)):
                expert_tiles(rare, expert[RARE:])
                pe.wait_ge(rare.y_copied, rare.n)
            keep_warm(8)
            expert_tiles(main, expert[:RARE] + list(range(E)))

        @block.scalar
        def _(act):
            act.dma_start(w1_all[:], w1.rearrange("l h a -> h l a")).then_inc(w1_in, 16)
            act.wait_ge(warm_set, 2)
            nc.scalar.activation(std[:, 0:1], eps[:], ACT.Sqrt)
            for g in range(GROUPS):
                act.wait_ge(xT_ps, g + 1)
                nc.scalar.activation(xT[:, g * GB:(g + 1) * GB, :], bank[g][:], ACT.Copy).then_inc(xT_done, 1)
            act.wait_ge(params_done, 1)
            for g in range(GROUPS):
                act.wait_ge(hT_ps, 2 * g + 1)
                for b in range(g * GB, (g + 1) * GB, 2):
                    nc.scalar.activation(hT[0:A, b, :], h_place(b), ACT.Relu,
                                         bias=params[0:A, 2 * B + b:2 * B + b + 1]).then_inc(hT_even, 1)
            for g in range(GROUPS):
                act.wait_ge(mv_done, (g + 1) * GB)
                nc.scalar.activation(std[:, g * GB:(g + 1) * GB], mv[:, g * GB:(g + 1) * GB, 1], ACT.Sqrt, bias=eps[:]
                                     ).then_inc(std_done, 1)
            act.wait_ge(std_done, GROUPS)
            nc.scalar.activation(half_tanh[:, 0:1], eps[:], ACT.Silu)
            act.wait_ge(params_done, 2)
            for b in (0, 1, 2, 3, 6, 7):
                act.wait_ge(zT_ps, 1 if b < GB else 3)
                at = bank[0][:, b * S:(b + 1) * S] if b < GB else bank[6][:, (b - 6) * S:(b - 5) * S]
                nc.scalar.activation(nT[:, b, :], at, ACT.Identity,
                                     scale=params[:, b:b + 1], bias=params[:, B + b:B + b + 1]).then_inc(nT_act, 1)
            def gate_silu(i):
                n = (SEGMENTS[i // K2][1] - SEGMENTS[i // K2][0]) * S
                act.wait_ge(sg_ps, i + 1)
                if i >= 2:
                    act.wait_ge(hs_done, i - 1)
                nc.scalar.activation(sg[:, i % 2, 0:n], bank[SH_BANKS[i % K2][0]][:, 0:n], ACT.Silu).then_inc(sg_done, 1)

            def scale_rows(b):
                act.wait_ge(n_ps, b // GB + 1)
                nc.scalar.activation(x_rows[:, b, 0:H], bank[3 + 3 * (b // GB)][:, (b % GB) * H:(b % GB + 1) * H],
                                     ACT.Copy, scale=score[:, b:b + 1]).then_inc(scaled, 1)

            act.wait_ge(top_done, 1)
            nc.scalar.activation(half_tanh[:], top[:], ACT.Tanh, scale=0.5).then_inc(tanh_done, 1)
            act.wait_ge(score_done, 1)
            for b in range(B):
                scale_rows(b)
            for i in range(K2 * len(SEGMENTS)):
                gate_silu(i)

            def expert_tiles(run):
                def x_evacuate(i):
                    act.wait_ge(run.exT_ps, i + 1)
                    if i >= 2:
                        act.wait_ge(run.gu_ps, i - 1)
                    nc.scalar.activation(exT[:, i % 2, :], bank[EX_X[i % 2]][:, 0:P], ACT.Copy).then_inc(run.exT_done, 1)

                x_evacuate(0)
                for i in range(run.n):
                    if i + 1 < run.n:
                        x_evacuate(i + 1)
                    act.wait_ge(run.gu_ps, i + 1)
                    if i >= 2:
                        act.wait_ge(run.eh_done, i - 1)
                    nc.scalar.activation(eg[:, i % 2, :], bank[EX_GU[i % 2]][:, 0:FF], ACT.Silu).then_inc(run.eg_done, 1)

            with nc.scalar.If(rare_in_use(nc.scalar)):
                expert_tiles(rare)
                act.wait_ge(rare.eh_done, rare.n)
            expert_tiles(main)

        @block.vector
        def _(dve):
            nc.vector.memset(warm[:], 0.0).then_inc(warm_set, 1)
            nc.vector.memset(eps[:], LN_EPS).then_inc(warm_set, 1)
            nc.vector.memset(hT[A:A + 1, :, :], 1.0).then_inc(dve_const, 1)
            nc.vector.memset(empty_row[:], 0.0).then_inc(dve_const, 1)
            dve.wait_ge(dve_const, 2)
            nc.vector.memset(empty_row[:, H:ROW].bitcast(I32), NO_TOKEN).then_inc(dve_const, 1)
            nc.vector.memset(ones[:], 1.0).then_inc(dve_const, 1)
            dve.wait_ge(ids_in, 16)
            dve.wait_ge(pool_const, 3)
            nc.vector.tensor_scalar(lang_hot[:], ids_sb[:], lang_no[0:L, :], None, ALU.is_equal).then_inc(lang_hot_done, 1)
            lang = load_numbers(nc.vector, ids_sb, B, L - 1)
            dve.wait_ge(w1_in, 16)
            for b in range(1, B, 2):
                nc.vector.tensor_copy(w1_sel[:, b:b + 1, :], w1_all[:, bass.ds(lang[b], 1), :]).then_inc(w1_odd, 1)
            dve.wait_ge(params_ps, 1)
            nc.vector.tensor_copy(params[0:A, 2 * B:3 * B], bank[0][0:A, 2 * B:3 * B]).then_inc(params_done, 1)
            dve.wait_ge(params_done, 1)
            for g in range(GROUPS):
                dve.wait_ge(hT_ps, 2 * g + 2)
                for b in range(g * GB + 1, (g + 1) * GB, 2):
                    nc.vector.tensor_scalar(hT[0:A, b, :], h_place(b), params[0:A, 2 * B + b:2 * B + b + 1], 0.0,
                                            ALU.add, ALU.max).then_inc(hT_odd, 1)

            def statistics(g):
                dve.wait_ge(v_ps, g + 1)
                for b in range(g * GB, (g + 1) * GB):
                    nc.vector.bn_stats(stats[:, b, :], bank[4 + g][:, (b % GB) * H:(b % GB + 1) * H]
                                       ).then_inc(stats_done, 1)
                for b in range(g * GB, (g + 1) * GB):
                    dve.wait_ge(stats_done, b + 1)
                    nc.vector.bn_aggr(mv[:, b, :], stats[:, b, :]).then_inc(mv_done, 1)

            def normalize(g):
                dve.wait_ge(std_done, g + 1)
                nc.vector.reciprocal(rstd[:, g * GB:(g + 1) * GB], std[:, g * GB:(g + 1) * GB]).then_inc(rstd_done, 1)
                dve.wait_ge(rstd_done, g + 1)
                for b in range(g * GB, (g + 1) * GB):
                    nc.vector.tensor_scalar(z[:, b, :], bank[4 + g][:, (b % GB) * H:(b % GB + 1) * H],
                                            mv[:, b, 0:1], rstd[:, b:b + 1], ALU.subtract, ALU.mult).then_inc(z_done, 1)

            statistics(0)
            statistics(1)
            normalize(0)
            dve.wait_ge(params_ps, 2)
            nc.vector.tensor_copy(params[:, 0:2 * B], bank[1][:, 0:2 * B])
            nc.vector.tensor_copy(params[:, 3 * B:3 * B + E], bank[1][:, 3 * B:3 * B + E]).then_inc(params_done, 1)
            normalize(1)
            dve.wait_ge(params_done, 2)
            dve.wait_ge(zT_ps, 2)
            for b in (4, 5):
                nc.vector.tensor_scalar(nT[:, b, :], bank[1][:, (b - 4) * S:(b - 3) * S],
                                        params[:, b:b + 1], params[:, B + b:B + b + 1], ALU.mult, ALU.add
                                        ).then_inc(nT_dve, 1)

            def shared_hidden(i):
                (a, b), k = SEGMENTS[i // K2], i % K2
                dve.wait_ge(sg_done, i + 1)
                dve.wait_ge(su_ps, i + 1)
                nc.vector.tensor_tensor(hs[:, k, a * S:b * S], sg[:, i % 2, 0:(b - a) * S],
                                        bank[SH_BANKS[k][1]][:, 0:(b - a) * S], ALU.mult).then_inc(hs_done, 1)

            def residual(s):
                for b in range(*SEGMENTS[s]):
                    dve.wait_ge(sd_ps, b + 1)
                    nc.vector.tensor_tensor(r_rows[:, b, :], bank[(3, 2)[b % 2]][:, 0:H], x_tok[:, b, :], ALU.add
                                            ).then_inc(r_done, 1)

            dve.wait_ge(logits_ps, 1)
            dve.wait_ge(pool_const, 12)
            logits = bank[2][:, 0:B * E].rearrange("p (b e) -> p b e", b=B)
            nc.vector.tensor_reduce(top[:], logits, AX_X, ALU.max).then_inc(top_done, 1)
            dve.wait_ge(top_done, 1)
            nc.vector.tensor_tensor(is_top[:], logits, top[:].unsqueeze(2).to_broadcast([P, B, E]),
                                    ALU.is_equal).then_inc(route, 1)
            dve.wait_ge(route, 1)
            nc.vector.tensor_tensor(ranked[:], is_top[:], rev[:].unsqueeze(1).to_broadcast([P, B, E]),
                                    ALU.mult).then_inc(route, 1)
            dve.wait_ge(tanh_done, 1)
            nc.vector.tensor_scalar(score[:], half_tanh[:], 0.5, 0.5, ALU.mult, ALU.add).then_inc(score_done, 1)
            dve.wait_ge(route, 2)
            nc.vector.tensor_reduce(first[:], ranked[:], AX_X, ALU.max).then_inc(route, 1)
            dve.wait_ge(route, 3)
            nc.vector.tensor_tensor(hot[:], ranked[:], first[:].unsqueeze(2).to_broadcast([P, B, E]),
                                    ALU.is_equal).then_inc(hot_done, 1)
            nc.vector.tensor_scalar(base[:], first[:], -float(P), float(P * E), ALU.mult, ALU.add).then_inc(route, 1)
            dve.wait_ge(count_ps, 1)
            nc.vector.tensor_scalar(over_k[:], thresholds[:], bank[5][0:E, COUNT:COUNT + 1], None, ALU.is_lt, ALU.add,
                                    accum_out=over_n[:]).then_inc(over_n_done, 1)
            dve.wait_ge(pos_ps, 1)
            dve.wait_ge(hot_done, 1)
            before_me = bank[2][:, 0:B * E].rearrange("p (b e) -> p b e", b=B)
            nc.vector.tensor_tensor(place_hot[:], before_me, hot[:], ALU.mult).then_inc(pos_read, 1)
            dve.wait_ge(pos_read, 1)
            nc.vector.tensor_reduce(place[:], place_hot[:], AX_X, ALU.add).then_inc(route, 1)
            dve.wait_ge(route, 5)
            nc.vector.tensor_tensor(slot_fix[:], place[:], base[:], ALU.add).then_inc(route, 1)
            dve.wait_ge(shift_ps, 1)
            nc.vector.tensor_tensor(shift_hot[:], hot[:], bank[5][:, 0:E].unsqueeze(1).to_broadcast([P, B, E]),
                                    ALU.mult).then_inc(route, 1)
            dve.wait_ge(route, 7)
            nc.vector.tensor_reduce(shift[:], shift_hot[:], AX_X, ALU.add).then_inc(route, 1)
            dve.wait_ge(route, 8)
            nc.vector.scalar_tensor_tensor(out=shifted[:], in0=place[:], scalar=float(P), in1=shift[:],
                                           op0=ALU.is_ge, op1=ALU.mult).then_inc(route, 1)
            dve.wait_ge(route, 9)
            nc.vector.tensor_tensor(slot[:], slot_fix[:], shifted[:], ALU.add).then_inc(slot_done, 1)
            nc.vector.tensor_tensor(past[:], bank[5][0:1, 1:E].unsqueeze(1).to_broadcast([1, OVER, E - 1]), bounds[:],
                                    ALU.is_le).then_inc(route, 1)
            dve.wait_ge(route, 10)
            nc.vector.tensor_reduce(over_ex_f[:], past[:], AX_X, ALU.add).then_inc(route, 1)
            dve.wait_ge(route, 11)
            nc.vector.tensor_copy(over_ex[:], over_ex_f[:]).then_inc(over_ex_done, 1)
            nc.vector.tensor_copy(over_size[:], bank[5][0:1, E:E + 1]).then_inc(over_ex_done, 1)
            for s in range(len(SEGMENTS)):
                for k in range(K2):
                    shared_hidden(s * K2 + k)
                residual(s)

            def expert_tiles(run):
                def gated(i):
                    dve.wait_ge(run.eg_done, i + 1)
                    if i >= 3:
                        dve.wait_ge(run.ehT_ps if i - 3 < run.over else run.y_ps, i - 2)
                    nc.vector.tensor_tensor(eh[:, i % 3, :], eg[:, i % 2, :], bank[EX_GU[i % 2]][:, FF:2 * FF],
                                            ALU.mult).then_inc(run.eh_done, 1)

                def y_copy(i):
                    dve.wait_ge(run.y_ps, i + 1)
                    nc.vector.tensor_copy(y[:, run.tiles[i], :], bank[EX_Y[i % 2]][:, 0:H]).then_inc(run.y_copied, 1)

                def add_r(i):
                    tile = run.tiles[i]
                    dve.wait_ge(run.y_copied, i + 1)
                    dve.wait_ge(slot_r_in[piece_of(tile)], 16)
                    nc.vector.tensor_tensor(y[:, tile, :], y[:, tile, :], slot_r[:, tile, :], ALU.add
                                            ).then_inc(run.y_done, 1)

                def h_evacuate(i):
                    dve.wait_ge(run.ehT_ps, i + 1)
                    if i >= 2:
                        dve.wait_ge(run.y_ps, i - 1)
                    nc.vector.tensor_copy(ehT[:, i % 2, :, :], bank[EX_H[i % 2]][:, 0:FF]).then_inc(run.ehT_done, 1)

                added = 0
                for i in range(run.n + 2):
                    if i >= 2:
                        y_copy(i - 2)
                    if i < run.n:
                        gated(i)
                    if 1 <= i <= run.over:
                        h_evacuate(i - 1)
                    if i >= run.lag:
                        for _ in range(min(2, i - 1 - added)):
                            add_r(added)
                            added += 1

            with nc.vector.If(rare_in_use(nc.vector)):
                expert_tiles(rare)
            expert_tiles(main)


_INS = ["x", "itok_B_0_8", "L0_cond_W1", "L0_cond_b1", "L0_cond_W2", "L0_cond_b2", "L0_cond_gamma", "L0_cond_beta",
        "L0_ffn_router_w", "L0_ffn_expert_gate", "L0_ffn_expert_up", "L0_ffn_expert_down",
        "L0_ffn_shared_gate", "L0_ffn_shared_up", "L0_ffn_shared_down"]


def kernel(**inputs):
    import numpy as _np
    import concourse.bacc as _bacc
    from concourse import mybir as _mybir
    from concourse.bass_utils import run_bass_kernel_spmd as _run

    nc = _bacc.Bacc("TRN2", target_bir_lowering=False, num_devices=1)
    arrays, args = {}, []
    for name in _INS:
        a = _np.ascontiguousarray(inputs[name])
        arrays[f"in_{name}_dram"] = a
        args.append(nc.dram_tensor(f"in_{name}_dram", a.shape, _mybir.dt.from_np(a.dtype), kind="ExternalInput").ap())
    out = nc.dram_tensor("out_dram", inputs["x"].shape, _mybir.dt.float32, kind="ExternalOutput").ap()
    adaln_moe_kernel(nc, *args, out)
    r = _run(nc, [arrays], core_ids=[0])
    return r.results[0]["out_dram"]
```

```python
from contextlib import ExitStack

import concourse.bass as bass
from concourse import mybir
from concourse.alu_op_type import AluOpType as ALU

P = 128
F32 = mybir.dt.float32
BF16 = mybir.dt.bfloat16
I32 = mybir.dt.int32
U32 = mybir.dt.uint32
ACT = mybir.ActivationFunctionType
AX_X = mybir.AxisListType.X

LN_EPS = 1e-5


def adaln_moe_kernel(nc, x, ids, w1, b1, w2, b2, gamma, beta, router_w,
                     expert_gate, expert_up, expert_down, shared_gate, shared_up, shared_down, out):
    B, S, H = x.shape
    L, _, A = w1.shape
    E, _, FF = expert_gate.shape
    K2 = FF // P
    T = B * S
    assert S == P and H == P and K2 == 2
    GROUPS = 2
    GB = B // GROUPS
    OVER = (T - P) // P
    TILES = E + OVER
    RARE = 4
    FIRST, KEPT, USED = 0, E, 2 * E
    AGAIN = 2 * E + 1
    ALL = AGAIN + E
    COUNT = ALL + 1
    ROW = H + 1

    SEGMENTS = [(0, 4), (4, B)]
    NO_TOKEN = 4 * T

    slots_x = nc.dram_tensor("slots_x", (TILES * P, ROW), F32, kind="Internal").ap()
    slots_r = nc.dram_tensor("slots_r", (TILES * P, H), F32, kind="Internal").ap()
    out_rows = out.rearrange("b s h -> (b s) h")

    with ExitStack() as ctx:
        def sb(name, shape, dt=F32):
            return ctx.enter_context(nc.sbuf_tensor(name, shape, dt))

        def sem(name):
            return ctx.enter_context(nc.semaphore(name))

        bank = [ctx.enter_context(nc.psum_tensor(f"bank{i}", [P, 512], F32)) for i in range(8)]

        ident = sb("ident", [P, P])
        tri = sb("tri", [P, P], BF16)
        ones = sb("ones", [P, P], BF16)
        rev = sb("rev", [P, E])
        from_first = sb("from_first", [E, ALL], BF16)
        from_all = sb("from_all", [E, E + 1], BF16)
        behind = sb("behind", [1, E], BF16)
        thresholds = sb("thresholds", [E, OVER])
        bounds = sb("bounds", [1, OVER, E - 1])
        steps = sb("steps", [1, OVER])
        warm = sb("warm", [P, P], BF16)
        lang_no = sb("lang_no", [P, 1])
        empty_row = sb("empty_row", [P, ROW])
        x_tok = sb("x_tok", [P, B, H])
        ids_sb = sb("ids_sb", [L, B], I32)
        w1_all = sb("w1_all", [P, L, A])
        w2_all = sb("w2_all", [A + 1, L, H])
        b1_rows = sb("b1_rows", [L, A])
        gamma_rows = sb("gamma_rows", [L, H])
        beta_rows = sb("beta_rows", [L, H])
        rw_rows = sb("rw_rows", [E, H])
        gu_sh = sb("gu_sh", [P, 2, FF])
        down_sh = sb("down_sh", [P, K2, H])
        gu_ex = sb("gu_ex", [P, E, 2 * FF])
        down_ex = sb("down_ex", [P, E, K2, H])
        lang_hot = sb("lang_hot", [L, B])
        params = sb("params", [P, 3 * B + E])
        w1_sel = sb("w1_sel", [P, B, A])
        xT = sb("xT", [P, B, S])
        hT = sb("hT", [A + 1, B, S])
        stats = sb("stats", [P, B, 6])
        mv = sb("mv", [P, B, 2])
        std = sb("std", [P, B])
        eps = sb("eps", [P, 1])
        rstd = sb("rstd", [P, B])
        z = sb("z", [P, B, H])
        nT = sb("nT", [P, B, S])
        top = sb("top", [P, B])
        half_tanh = sb("half_tanh", [P, B])
        score = sb("score", [P, B])
        is_top = sb("is_top", [P, B, E])
        ranked = sb("ranked", [P, B, E])
        first = sb("first", [P, B])
        hot = sb("hot", [P, B, E], BF16)
        over_k = sb("over_k", [E, OVER])
        over_n = sb("over_n", [E, GROUPS], BF16)
        base = sb("base", [P, B])
        place_hot = sb("place_hot", [P, B, E])
        place = sb("place", [P, B])
        slot_fix = sb("slot_fix", [P, B])
        shift_hot = sb("shift_hot", [P, B, E])
        shift = sb("shift", [P, B])
        shifted = sb("shifted", [P, B])
        table = sb("table", [P, AGAIN])
        pair_hot = sb("pair_hot", [P, GB, 2, E])
        pair = sb("pair", [P, GB, 2])
        beyond = sb("beyond", [P, GB])
        slot_near = sb("slot_near", [P, GB])
        slot = sb("slot", [P, B], U32)
        starts = sb("starts", [1, E])
        starts_kept = sb("starts_kept", [1, E])
        past = sb("past", [1, OVER, 2, E - 1])
        past_sum = sb("past_sum", [1, OVER])
        own = sb("own", [1, OVER])
        over_ex_f = sb("over_ex_f", [1, OVER])
        over_size = sb("over_size", [1, 1], I32)
        over_ex = sb("over_ex", [1, OVER], I32)
        x_rows = sb("x_rows", [P, B, ROW])
        sg = sb("sg", [P, 2, 512])
        hs = sb("hs", [P, K2, T])
        r_rows = sb("r_rows", [P, B, H])
        slot_x = sb("slot_x", [P, TILES, ROW])
        slot_r = sb("slot_r", [P, TILES, H])
        exT = sb("exT", [P, 2, P])
        eg = sb("eg", [P, 2, FF])
        eh = sb("eh", [P, 3, FF])
        ehT = sb("ehT", [P, 2, K2, P])
        y = sb("y", [P, TILES, H])

        x_in = [sem(f"x_in{i}") for i in range(2)]
        ids_in, b1_in, w1_in, w2_in, par_in = sem("ids_in"), sem("b1_in"), sem("w1_in"), sem("w2_in"), sem("par_in")
        sh_in, gu_in, down_in = sem("sh_in"), sem("gu_in"), sem("down_in")
        pool_const, dve_const = sem("pool_const"), sem("dve_const")
        lang_hot_done, params_ps, params_done = sem("lang_hot_done"), sem("params_ps"), sem("params_done")
        w1_even, w1_odd, xT_ps, xT_done = sem("w1_even"), sem("w1_odd"), sem("xT_ps"), sem("xT_done")
        hT_ps, hT_act, hT_dve, v_ps = sem("hT_ps"), sem("hT_act"), sem("hT_dve"), sem("v_ps")
        stats_done, mv_done, std_done, rstd_done = sem("stats_done"), sem("mv_done"), sem("std_done"), sem("rstd_done")
        z_done, zT_ps, nT_done = sem("z_done"), sem("zT_ps"), sem("nT_done")
        logits_ps, top_done, tanh_done, score_done = sem("logits_ps"), sem("top_done"), sem("tanh_done"), sem("score_done")
        route = [sem(f"route{g}") for g in range(GROUPS)]
        hot_done, pos_ps, pos_read, table_done = sem("hot_done"), sem("pos_ps"), sem("pos_read"), sem("table_done")
        count_ps, over_n_done, shift_ps, warm_set = sem("count_ps"), sem("over_n_done"), sem("shift_ps"), sem("warm_set")
        slot_done, over_ex_done = sem("slot_done"), sem("over_ex_done")
        n_ps, scaled = sem("n_ps"), sem("scaled")
        fill_x, fill_r, x_out, r_out = sem("fill_x"), sem("fill_r"), sem("x_out"), sem("r_out")
        sg_ps, su_ps, sg_done, hs_done = sem("sg_ps"), sem("su_ps"), sem("sg_done"), sem("hs_done")
        sd_ps, r_done = sem("sd_ps"), sem("r_done")
        PIECES = [(E, E + 1), (E + 1, E + RARE), (0, 3), (3, E), (E + RARE, TILES)]
        slot_x_in = [sem(f"slot_x_in{i}") for i in range(len(PIECES))]
        slot_r_in = [sem(f"slot_r_in{i}") for i in range(len(PIECES))]

        class Run:
            def __init__(self, name, tiles, lag, copied):
                self.lag = lag
                self.copied = copied
                self.tiles = tiles
                self.n = len(tiles)
                self.over = sum(t >= E for t in tiles)
                self.exT_ps, self.exT_done = sem(f"{name}_exT_ps"), sem(f"{name}_exT_done")
                self.gu_ps, self.eg_done, self.eh_done = sem(f"{name}_gu_ps"), sem(f"{name}_eg_done"), sem(f"{name}_eh_done")
                self.ehT_ps, self.ehT_done = sem(f"{name}_ehT_ps"), sem(f"{name}_ehT_done")
                self.y_ps, self.y_copied = sem(f"{name}_y_ps"), sem(f"{name}_y_copied")
                self.y_done, self.y_out = sem(f"{name}_y_done"), sem(f"{name}_y_out")

        rare = Run("rare", list(range(E + RARE, TILES)), lag=2, copied=1)
        main = Run("main", list(range(E, E + RARE)) + list(range(E)), lag=4, copied=4)

        def rare_in_use(engine):
            engine.wait_ge(over_ex_done, 2)
            return engine.value_load(over_size[0:1, 0:1], min_val=0, max_val=P * OVER) > P * RARE

        def piece_of(j):
            return next(i for i, (a, b) in enumerate(PIECES) if a <= j < b)

        EX_X, EX_GU, EX_H, EX_Y = (2, 5), (0, 1), (4, 7), (3, 6)

        def z_place(b):
            bk, at = ((0, 0), (3, 0), (6, 0), (1, 0), (1, 1), (7, 0), (6, 1), (1, 2))[b]
            return bank[bk][:, at * S:(at + 1) * S]

        def v_place(b, end=None):
            bk, at = (4, b) if b < 2 else (1, b - 2) if b < GB else (5, b - GB)
            return bank[bk][:, at * H:(at + (end or b + 1) - b) * H]

        V_LAST = (1, 3, 7)

        N_ROWS = (3, 6)
        NUM = (2, 5)
        SH_Y = (3, 6, 4, 5)
        SH_BANKS = [(0, 7), (1, 2)]

        def h_place(b):
            bk = bank[(2, 3, 6, 7)[2 * (b // GB) + b % 2]]
            at = (b % GB) // 2
            return bk[0:A, at * S:(at + 1) * S]

        RELU_ORDER = ((0, 1, 2, 3), (4, 6, 5, 7))

        def relu_done(b):
            return (hT_dve, b // 2 + 1) if b in (1, 3) else (hT_act, (0, 2, 4, 6, 5, 7).index(b) + 1)

        def load_numbers(engine, row, n, high):
            values = []
            for i in range(0, n, 4):
                regs = [engine.alloc_register(f"{row.name}_{k}") for k in range(i, min(i + 4, n))]
                engine.reg_load(regs, row[0:1, i:i + len(regs)])
                values += [engine.snap(r, min_val=0, max_val=high) for r in regs]
            return values

        block = ctx.enter_context(nc.Block())

        @block.sync
        def _(sp):
            xr = x.rearrange("b s h -> s b h")
            sp.dma_start(x_tok[:, 0:GB, :], xr[:, 0:GB, :]).then_inc(x_in[0], 16)
            sp.dma_start(ids_sb[:], ids.rearrange("(a b) -> a b", a=1).to_broadcast([L, B])).then_inc(ids_in, 16)
            sp.dma_start(x_tok[:, GB:B, :], xr[:, GB:B, :]).then_inc(x_in[1], 16)
            sp.dma_start(b1_rows[:], b1).then_inc(b1_in, 16)
            sp.dma_start(w2_all[0:A, :, :], w2.rearrange("l a h -> a l h")).then_inc(w2_in, 16)
            sp.dma_start(w2_all[A:A + 1, :, :], b2.rearrange("(a l) h -> a l h", a=1)).then_inc(w2_in, 16)
            sp.dma_start(gamma_rows[:], gamma).then_inc(par_in, 16)
            sp.dma_start(beta_rows[:], beta).then_inc(par_in, 16)
            sp.dma_start(rw_rows[:], router_w).then_inc(par_in, 16)
            sp.dma_start(gu_sh[:, 0, :], shared_gate).then_inc(sh_in, 16)
            sp.dma_start(gu_sh[:, 1, :], shared_up).then_inc(sh_in, 16)
            sp.dma_start(down_sh[:], shared_down.rearrange("(k p) h -> p k h", p=P)).then_inc(sh_in, 16)
            sp.wait_ge(dve_const, 3)
            sp.dma_start(slots_x.rearrange("(j p) w -> p j w", p=P),
                         empty_row[:].unsqueeze(1).to_broadcast([P, TILES, ROW])).then_inc(fill_x, 16)
            sp.dma_start(slots_r.rearrange("(j p) h -> p j h", p=P),
                         empty_row[:, 0:H].unsqueeze(1).to_broadcast([P, TILES, H])).then_inc(fill_r, 16)
            sp.dma_start(gu_ex[:, :, 0:FF], expert_gate.rearrange("e d f -> d e f")).then_inc(gu_in, 16)
            sp.dma_start(gu_ex[:, :, FF:2 * FF], expert_up.rearrange("e d f -> d e f")).then_inc(gu_in, 16)
            sp.dma_start(down_ex[:], expert_down.rearrange("e (k p) h -> p e k h", p=P)).then_inc(down_in, 16)
            sp.wait_ge(x_out, 16 * B)
            for i, (a, b) in enumerate(PIECES):
                sp.dma_start(slot_x[:, a:b, :], slots_x[a * P:b * P, :].rearrange("(j p) w -> p j w", p=P)
                             ).then_inc(slot_x_in[i], 16)
            sp.wait_ge(r_out, 16 * B)
            for i, (a, b) in enumerate(PIECES):
                sp.dma_start(slot_r[:, a:b, :], slots_r[a * P:b * P, :].rearrange("(j p) h -> p j h", p=P)
                             ).then_inc(slot_r_in[i], 16)

        @block.gpsimd
        def _(pool):
            nc.gpsimd.memset(ident[:], 0.0).then_inc(pool_const, 1)
            pool.wait_ge(pool_const, 1)
            nc.gpsimd.affine_select(out=ident[:], in_=ident[:], compare_op=ALU.not_equal, fill=1.0, base=0,
                                    pattern=[[-1, P]], channel_multiplier=1).then_inc(pool_const, 1)
            nc.gpsimd.iota(lang_no[:], [[0, 1]], base=0, channel_multiplier=1,
                           allow_small_or_imprecise_dtypes=True).then_inc(pool_const, 1)
            pool.wait_ge(ids_in, 16)
            lang = load_numbers(nc.gpsimd, ids_sb, B, L - 1)
            pool.wait_ge(w1_in, 16)
            for b in range(0, B, 2):
                nc.gpsimd.tensor_copy(w1_sel[:, b:b + 1, :], w1_all[:, bass.ds(lang[b], 1), :]).then_inc(w1_even, 1)
            nc.gpsimd.memset(tri[:], 1.0).then_inc(pool_const, 1)
            nc.gpsimd.memset(from_first[:, FIRST:E], float(P)).then_inc(pool_const, 1)
            nc.gpsimd.memset(from_first[:, KEPT:KEPT + E], 0.0).then_inc(pool_const, 1)
            nc.gpsimd.memset(from_first[:, USED:USED + 1], float(P)).then_inc(pool_const, 1)
            nc.gpsimd.memset(from_first[:, AGAIN:ALL], -float(P)).then_inc(pool_const, 1)
            nc.gpsimd.memset(from_all[:], float(P)).then_inc(pool_const, 1)
            pool.wait_ge(pool_const, 9)
            nc.gpsimd.affine_select(out=tri[:], in_=tri[:], compare_op=ALU.is_gt, fill=0.0, base=0,
                                    pattern=[[1, P]], channel_multiplier=-1).then_inc(pool_const, 1)
            nc.gpsimd.affine_select(out=from_first[:, FIRST:E], in_=from_first[:, FIRST:E], compare_op=ALU.is_gt,
                                    fill=0.0, base=0, pattern=[[1, E]], channel_multiplier=-1).then_inc(pool_const, 1)
            nc.gpsimd.affine_select(out=from_first[:, KEPT:KEPT + E], in_=from_first[:, KEPT:KEPT + E],
                                    compare_op=ALU.not_equal, fill=float(P), base=0, pattern=[[1, E]],
                                    channel_multiplier=-1).then_inc(pool_const, 1)
            nc.gpsimd.affine_select(out=from_first[:, AGAIN:ALL], in_=from_first[:, AGAIN:ALL], compare_op=ALU.is_gt,
                                    fill=float(P), base=0, pattern=[[1, E]], channel_multiplier=-1).then_inc(pool_const, 1)
            pool.wait_ge(pool_const, 13)
            nc.gpsimd.affine_select(out=from_first[:, AGAIN:ALL], in_=from_first[:, AGAIN:ALL],
                                    compare_op=ALU.not_equal, fill=0.0, base=0, pattern=[[1, E]],
                                    channel_multiplier=-1).then_inc(pool_const, 1)
            nc.gpsimd.affine_select(out=from_all[:], in_=from_all[:], compare_op=ALU.is_gt, fill=0.0, base=0,
                                    pattern=[[1, E + 1]], channel_multiplier=-1).then_inc(pool_const, 1)
            nc.gpsimd.iota(rev[:], [[-1, E]], base=E, channel_multiplier=0,
                           allow_small_or_imprecise_dtypes=True).then_inc(pool_const, 1)
            nc.gpsimd.iota(behind[:], [[-P, E]], base=P * (E - 1), channel_multiplier=0,
                           allow_small_or_imprecise_dtypes=True).then_inc(pool_const, 1)
            nc.gpsimd.iota(thresholds[:], [[P, OVER]], base=P, channel_multiplier=0,
                           allow_small_or_imprecise_dtypes=True).then_inc(pool_const, 1)
            nc.gpsimd.iota(bounds[:], [[P, OVER], [-P, E - 1]], base=P * (E - 2), channel_multiplier=0,
                           allow_small_or_imprecise_dtypes=True).then_inc(pool_const, 1)
            nc.gpsimd.iota(steps[:], [[P, OVER]], base=0, channel_multiplier=0,
                           allow_small_or_imprecise_dtypes=True).then_inc(pool_const, 1)
            nc.gpsimd.iota(x_rows[:, :, H].bitcast(I32), [[P, B]], base=0, channel_multiplier=1).then_inc(pool_const, 1)
            pool.wait_ge(pool_const, 21)
            pool.wait_ge(fill_x, 16)
            for b in range(B):
                pool.wait_ge(slot_done, b // GB + 1)
                pool.wait_ge(scaled, b + 1)
                nc.gpsimd.indirect_dma_start(
                    out=slots_x, out_offset=bass.IndirectOffsetOnAxis(ap=slot[:, b:b + 1], axis=0),
                    in_=x_rows[:, b, :], in_offset=None).then_inc(x_out, 16)
            pool.wait_ge(fill_r, 16)
            for b in range(B):
                pool.wait_ge(r_done, b + 1)
                nc.gpsimd.indirect_dma_start(
                    out=slots_r, out_offset=bass.IndirectOffsetOnAxis(ap=slot[:, b:b + 1], axis=0),
                    in_=r_rows[:, b, :], in_offset=None).then_inc(r_out, 16)
            def tiles_out(run):
                for i, tile in enumerate(run.tiles):
                    pool.wait_ge(slot_x_in[piece_of(tile)], 16)
                    pool.wait_ge(run.y_done, i + 1)
                    nc.gpsimd.indirect_dma_start(
                        out=out_rows,
                        out_offset=bass.IndirectOffsetOnAxis(ap=slot_x[:, tile, H:H + 1].bitcast(U32), axis=0),
                        in_=y[:, tile, :], in_offset=None, bounds_check=T - 1, oob_is_err=False,
                    ).then_inc(run.y_out, 16)
                pool.wait_ge(run.y_out, 16 * run.n)

            with nc.gpsimd.If(rare_in_use(nc.gpsimd)):
                tiles_out(rare)
            tiles_out(main)
            pool.wait_ge(slot_x_in[-1], 16)
            pool.wait_ge(slot_r_in[-1], 16)

        @block.tensor
        def _(pe):
            def keep_warm(n, blocks=4):
                for _ in range(n):
                    nc.tensor.matmul(bank[7][:, 0:blocks * P], warm[:], warm[:].unsqueeze(1).to_broadcast([P, blocks, P]),
                                     start=True, stop=True)

            def turn_z(b):
                pe.wait_ge(z_done, b + 1)
                nc.tensor.transpose(z_place(b), z[:, b, :], ident[:]).then_inc(zT_ps, 1)

            def turn_tokens(g):
                pe.wait_ge(x_in[g], 16)
                for b in range(g * GB, (g + 1) * GB):
                    last = nc.tensor.transpose(bank[g][:, (b % GB) * S:(b % GB + 1) * S], x_tok[:, b, :], ident[:])
                last.then_inc(xT_ps, 1)

            def start_v(first, end):
                nc.tensor.matmul(v_place(first, end), ident[:], x_tok[:, first:end, :], start=True, stop=False,
                                 skip_group_check=True)

            def adapter_down(g):
                pe.wait_ge(xT_done, g + 1)
                for b in [*range(g * GB, (g + 1) * GB, 2), *range(g * GB + 1, (g + 1) * GB, 2)]:
                    pe.wait_ge(w1_odd if b % 2 else w1_even, b // 2 + 1)
                    last = nc.tensor.matmul(h_place(b), w1_sel[:, b, :], xT[:, b, :], start=True, stop=True)
                    if b % GB >= GB - 2:
                        last.then_inc(hT_ps, 1)

            def adapter_up(b):
                pe.wait_ge(*relu_done(b))
                last = nc.tensor.matmul(v_place(b), hT[:, b, :], w2_all[:, bass.ds(lang[b], 1), :], start=False,
                                        stop=(b in V_LAST), skip_group_check=True)
                if b in V_LAST:
                    last.then_inc(v_ps, 1)

            pe.wait_ge(warm_set, 1)
            keep_warm(8)
            pe.wait_ge(pool_const, 2)
            turn_tokens(0)
            turn_tokens(1)
            lang = load_numbers(nc.tensor, ids_sb, B, L - 1)
            pe.wait_ge(b1_in, 16)
            pe.wait_ge(lang_hot_done, 1)
            nc.tensor.matmul(bank[6][0:A, 0:B], b1_rows[:], lang_hot[:], start=True, stop=True).then_inc(params_ps, 1)
            adapter_down(0)
            start_v(0, 2)
            pe.wait_ge(xT_done, GROUPS)
            start_v(2, GB)
            pe.wait_ge(w2_in, 32)
            pe.wait_ge(dve_const, 1)
            for b in RELU_ORDER[0]:
                adapter_up(b)
            pe.wait_ge(par_in, 48)
            nc.tensor.matmul(bank[0][:, 0:B], gamma_rows[:], lang_hot[:], start=True, stop=True)
            nc.tensor.matmul(bank[0][:, B:2 * B], beta_rows[:], lang_hot[:], start=True, stop=True)
            nc.tensor.transpose(bank[0][:, 2 * B:2 * B + E], rw_rows[:], ident[0:E, 0:E]).then_inc(params_ps, 1)
            adapter_down(1)
            start_v(GB, B)
            pe.wait_ge(params_done, 2)
            for i in range(GB - 1):
                adapter_up(RELU_ORDER[1][i])
                turn_z(i)
            adapter_up(RELU_ORDER[1][GB - 1])

            def router(first, end):
                for b in range(first, end):
                    pe.wait_ge(nT_done, b + 1)
                    last = nc.tensor.matmul(bank[NUM[b // GB]][:, (b % GB) * E:(b % GB + 1) * E], nT[:, b, :],
                                            params[:, 3 * B:3 * B + E], start=True, stop=True)
                return last

            def shared_up(i, u, first=0, end=GB):
                (a, b), k = SEGMENTS[i // K2], i % K2
                if i >= 2:
                    pe.wait_ge(hs_done, i - 1)
                last = nc.tensor.matmul(bank[SH_BANKS[k][u]][:, first * S:end * S], gu_sh[:, u, k * P:(k + 1) * P],
                                        nT[:, a + first:a + end, :], start=True, stop=True)
                if end == GB:
                    last.then_inc(su_ps if u else sg_ps, 1)

            def shared_down(b):
                pe.wait_ge(hs_done, K2 * (b // GB + 1))
                pe.wait_ge(scaled, B)
                if b >= len(SH_Y):
                    pe.wait_ge(r_done, b - len(SH_Y) + 1)
                for k in range(K2):
                    last = nc.tensor.matmul(bank[SH_Y[b % len(SH_Y)]][:, 0:H], hs[:, k, b * S:(b + 1) * S],
                                            down_sh[:, k, :], start=(k == 0), stop=(k == K2 - 1))
                last.then_inc(sd_ps, 1)

            def turn_n(g):
                for b in range(g * GB, (g + 1) * GB):
                    last = nc.tensor.transpose(bank[N_ROWS[g]][:, (b % GB) * H:(b % GB + 1) * H], nT[:, b, :], ident[:])
                last.then_inc(n_ps, 1)

            def count(g):
                pe.wait_ge(hot_done, g + 1)
                for b in range(g * GB, (g + 1) * GB):
                    last = nc.tensor.matmul(bank[4][0:E, COUNT:COUNT + 1], hot[:, b, :], ones[:, 0:1],
                                            start=False, stop=False, skip_group_check=True)
                last.then_inc(count_ps, 1)

            def places(g):
                at = bank[NUM[g]]
                nc.tensor.matmul(at[:, 0:GB * E], tri[:], hot[:, g * GB:(g + 1) * GB, :], start=True, stop=False,
                                 skip_group_check=True)
                for b in range((g + 1) * GB - 1):
                    after = max(b + 1, g * GB) - g * GB
                    last = nc.tensor.matmul(at[:, after * E:GB * E], ones[:],
                                            hot[:, b:b + 1, :].to_broadcast([P, GB - after, E]),
                                            start=False, stop=(b == (g + 1) * GB - 2), skip_group_check=True)
                last.then_inc(pos_ps, 1)

            turn_z(GB - 1)
            keep_warm(1)
            router(0, GB).then_inc(logits_ps, 1)
            turn_n(0)
            pe.wait_ge(sh_in, 48)
            shared_up(0, 0, 0, 2)
            keep_warm(2)
            turn_z(4)
            turn_z(5)
            pe.wait_ge(pool_const, 21)
            pe.wait_ge(dve_const, 4)
            nc.tensor.matmul(bank[4][:, FIRST:FIRST + E], ones[0:1, :], behind[:], start=True, stop=False,
                             skip_group_check=True)
            count(0)
            places(0)
            pe.wait_ge(over_n_done, 1)
            nc.tensor.matmul(bank[4][:, 0:ALL], over_n[:, 0:1].to_broadcast([E, P]), from_first[:], start=False, stop=False,
                             skip_group_check=True).then_inc(shift_ps, 1)
            turn_z(6)
            shared_up(0, 0, 2, 4)
            pe.wait_ge(nT_done, 5)
            turn_z(7)
            router(4, B).then_inc(logits_ps, 1)
            shared_up(0, 1)
            turn_n(1)
            pe.wait_ge(table_done, 1)
            count(1)
            places(1)
            shared_up(1, 0)
            pe.wait_ge(over_n_done, 2)
            nc.tensor.matmul(bank[4][:, AGAIN:ALL + 1], over_n[:, 1:2].to_broadcast([E, P]), from_all[:], start=False,
                             stop=True, skip_group_check=True).then_inc(shift_ps, 1)
            shared_up(1, 1)
            for i in range(K2, K2 * len(SEGMENTS)):
                shared_up(i, 0)
                shared_up(i, 1)
            shared_down(0)
            rare_used = rare_in_use(nc.tensor)
            expert = load_numbers(nc.tensor, over_ex, OVER, E - 1)
            for b in range(1, B):
                shared_down(b)

            def expert_tiles(run, expert):
                def turn_x(i):
                    pe.wait_ge(slot_x_in[piece_of(run.tiles[i])], 16)
                    if i >= 2:
                        pe.wait_ge(run.exT_done, i - 1)
                    nc.tensor.transpose(bank[EX_X[i % 2]][:, 0:P], slot_x[:, run.tiles[i], 0:H], ident[:]
                                        ).then_inc(run.exT_ps, 1)

                def gate_up(i):
                    pe.wait_ge(run.exT_done, i + 1)
                    if i >= 2:
                        pe.wait_ge(run.eh_done, i - 1)
                    if i < run.over:
                        last = nc.tensor.matmul(bank[EX_GU[i % 2]][:], exT[:, i % 2, :],
                                                gu_ex[:, bass.ds(expert[i], 1), :], start=True, stop=True)
                    else:
                        for k in range(2 * K2):
                            last = nc.tensor.matmul(bank[EX_GU[i % 2]][:, k * P:(k + 1) * P],
                                                    gu_ex[:, expert[i], k * P:(k + 1) * P], exT[:, i % 2, :],
                                                    start=True, stop=True)
                    last.then_inc(run.gu_ps, 1)

                def turn_h(i):
                    pe.wait_ge(run.eh_done, i + 1)
                    if i >= 2:
                        pe.wait_ge(run.ehT_done, i - 1)
                    for k in range(K2):
                        last = nc.tensor.transpose(bank[EX_H[i % 2]][:, k * P:(k + 1) * P],
                                                   eh[:, i % 3, k * P:(k + 1) * P], ident[:])
                    last.then_inc(run.ehT_ps, 1)

                def down(i):
                    if i < run.over:
                        pe.wait_ge(run.ehT_done, i + 1)
                    else:
                        pe.wait_ge(run.eh_done, i + 1)
                    if i >= 2:
                        pe.wait_ge(*((run.y_copied, i - 1) if i - 2 < run.copied else (run.y_done, i - 1)))
                    for k in range(K2):
                        hidden = ehT[:, i % 2, k, :] if i < run.over else eh[:, i % 3, k * P:(k + 1) * P]
                        last = nc.tensor.matmul(bank[EX_Y[i % 2]][:, 0:H], hidden,
                                                down_ex[:, bass.ds(expert[i], 1), k, :],
                                                start=(k == 0), stop=(k == K2 - 1))
                    last.then_inc(run.y_ps, 1)

                turn_x(0)
                for i in range(run.n + 2):
                    if i + 1 < run.n:
                        turn_x(i + 1)
                    if i - 2 >= run.over:
                        down(i - 2)
                    if i < run.n:
                        gate_up(i)
                    if 0 <= i - 2 < run.over:
                        down(i - 2)
                    if 1 <= i <= run.over:
                        turn_h(i - 1)

            pe.wait_ge(r_done, B)
            pe.wait_ge(gu_in, 32)
            pe.wait_ge(down_in, 16)
            with nc.tensor.If(rare_used):
                expert_tiles(rare, expert[RARE:])
                pe.wait_ge(rare.y_done, rare.n)
            expert_tiles(main, expert[:RARE] + list(range(E)))

        @block.scalar
        def _(act):
            act.dma_start(w1_all[:], w1.rearrange("l h a -> h l a")).then_inc(w1_in, 16)
            act.wait_ge(warm_set, 2)
            nc.scalar.activation(std[:, 0:1], eps[:], ACT.Sqrt)

            def xT_evacuate(g):
                act.wait_ge(xT_ps, g + 1)
                nc.scalar.activation(xT[:, g * GB:(g + 1) * GB, :], bank[g][:], ACT.Copy).then_inc(xT_done, 1)

            def relu(b):
                nc.scalar.activation(hT[0:A, b, :], h_place(b), ACT.Relu, bias=params[0:A, b:b + 1]
                                     ).then_inc(hT_act, 1)

            def deviation(g):
                act.wait_ge(mv_done, (g + 1) * GB)
                nc.scalar.activation(std[:, g * GB:(g + 1) * GB], mv[:, g * GB:(g + 1) * GB, 1], ACT.Sqrt, bias=eps[:]
                                     ).then_inc(std_done, 1)

            def affine(b):
                act.wait_ge(zT_ps, b + 1)
                nc.scalar.activation(nT[:, b, :], z_place(b), ACT.Identity, scale=params[:, B + b:B + b + 1],
                                     bias=params[:, 2 * B + b:2 * B + b + 1]).then_inc(nT_done, 1)

            def half_tanhs(g):
                act.wait_ge(top_done, g + 1)
                nc.scalar.activation(half_tanh[:, g * GB:(g + 1) * GB], top[:, g * GB:(g + 1) * GB], ACT.Tanh, scale=0.5
                                     ).then_inc(tanh_done, 1)

            def gate_silu(i):
                n = (SEGMENTS[i // K2][1] - SEGMENTS[i // K2][0]) * S
                act.wait_ge(sg_ps, i + 1)
                if i >= 2:
                    act.wait_ge(hs_done, i - 1)
                nc.scalar.activation(sg[:, i % 2, 0:n], bank[SH_BANKS[i % K2][0]][:, 0:n], ACT.Silu).then_inc(sg_done, 1)

            def scale_rows(b):
                act.wait_ge(n_ps, b // GB + 1)
                act.wait_ge(score_done, b // GB + 1)
                nc.scalar.activation(x_rows[:, b, 0:H], bank[N_ROWS[b // GB]][:, (b % GB) * H:(b % GB + 1) * H],
                                     ACT.Copy, scale=score[:, b:b + 1]).then_inc(scaled, 1)

            xT_evacuate(0)
            xT_evacuate(1)
            act.wait_ge(params_done, 1)
            act.wait_ge(hT_ps, 1)
            relu(0)
            relu(2)
            deviation(0)
            act.wait_ge(hT_ps, 3)
            relu(4)
            relu(6)
            act.wait_ge(hT_ps, 4)
            relu(5)
            relu(7)
            act.wait_ge(params_done, 2)
            affine(0)
            affine(1)
            affine(2)
            affine(3)
            deviation(1)
            act.wait_ge(std_done, GROUPS)
            nc.scalar.activation(half_tanh[:, B - 1:B], eps[:], ACT.Silu)
            half_tanhs(0)
            affine(4)
            affine(5)
            scale_rows(0)
            affine(6)
            scale_rows(1)
            affine(7)
            scale_rows(2)
            scale_rows(3)
            gate_silu(0)
            half_tanhs(1)
            for b in range(GB, B):
                scale_rows(b)
            for i in range(1, K2 * len(SEGMENTS)):
                gate_silu(i)

            def expert_tiles(run):
                def x_evacuate(i):
                    act.wait_ge(run.exT_ps, i + 1)
                    if i >= 2:
                        act.wait_ge(run.gu_ps, i - 1)
                    nc.scalar.activation(exT[:, i % 2, :], bank[EX_X[i % 2]][:, 0:P], ACT.Copy).then_inc(run.exT_done, 1)

                def h_evacuate(i):
                    act.wait_ge(run.ehT_ps, i + 1)
                    if i >= 2:
                        act.wait_ge(run.y_ps, i - 1)
                    nc.scalar.activation(ehT[:, i % 2, :, :], bank[EX_H[i % 2]][:, 0:FF], ACT.Copy).then_inc(run.ehT_done, 1)

                x_evacuate(0)
                for i in range(run.n + 1):
                    if i + 1 < run.n:
                        x_evacuate(i + 1)
                    if i < run.n:
                        act.wait_ge(run.gu_ps, i + 1)
                        if i >= 2:
                            act.wait_ge(run.eh_done, i - 1)
                        nc.scalar.activation(eg[:, i % 2, :], bank[EX_GU[i % 2]][:, 0:FF], ACT.Silu
                                             ).then_inc(run.eg_done, 1)
                    if 1 <= i <= run.over:
                        h_evacuate(i - 1)

            with nc.scalar.If(rare_in_use(nc.scalar)):
                expert_tiles(rare)
                act.wait_ge(rare.eh_done, rare.n)
            expert_tiles(main)

        @block.vector
        def _(dve):
            nc.vector.memset(warm[:], 0.0).then_inc(warm_set, 1)
            nc.vector.memset(eps[:], LN_EPS).then_inc(warm_set, 1)
            nc.vector.memset(hT[A:A + 1, :, :], 1.0).then_inc(dve_const, 1)
            nc.vector.memset(empty_row[:], 0.0).then_inc(dve_const, 1)
            dve.wait_ge(dve_const, 2)
            nc.vector.memset(empty_row[:, H:ROW].bitcast(I32), NO_TOKEN).then_inc(dve_const, 1)
            nc.vector.memset(ones[:], 1.0).then_inc(dve_const, 1)
            dve.wait_ge(ids_in, 16)
            dve.wait_ge(pool_const, 3)
            nc.vector.tensor_scalar(lang_hot[:], ids_sb[:], lang_no[0:L, :], None, ALU.is_equal).then_inc(lang_hot_done, 1)
            lang = load_numbers(nc.vector, ids_sb, B, L - 1)
            dve.wait_ge(w1_in, 16)
            for b in range(1, B, 2):
                nc.vector.tensor_copy(w1_sel[:, b:b + 1, :], w1_all[:, bass.ds(lang[b], 1), :]).then_inc(w1_odd, 1)
            dve.wait_ge(params_ps, 1)
            nc.vector.tensor_copy(params[0:A, 0:B], bank[6][0:A, 0:B]).then_inc(params_done, 1)
            dve.wait_ge(params_done, 1)

            def statistics(g):
                for b in range(g * GB, (g + 1) * GB):
                    dve.wait_ge(v_ps, sum(c < b for c in V_LAST) + 1)
                    nc.vector.bn_stats(stats[:, b, :], v_place(b)).then_inc(stats_done, 1)
                for b in range(g * GB, (g + 1) * GB):
                    dve.wait_ge(stats_done, b + 1)
                    nc.vector.bn_aggr(mv[:, b, :], stats[:, b, :]).then_inc(mv_done, 1)

            def deviation(g):
                dve.wait_ge(std_done, g + 1)
                nc.vector.reciprocal(rstd[:, g * GB:(g + 1) * GB], std[:, g * GB:(g + 1) * GB]).then_inc(rstd_done, 1)

            def normalize(b):
                dve.wait_ge(rstd_done, b // GB + 1)
                nc.vector.tensor_scalar(z[:, b, :], v_place(b), mv[:, b, 0:1], rstd[:, b:b + 1],
                                        ALU.subtract, ALU.mult).then_inc(z_done, 1)

            for b in range(1, GB, 2):
                dve.wait_ge(hT_ps, 2)
                nc.vector.tensor_scalar(hT[0:A, b, :], h_place(b), params[0:A, b:b + 1], 0.0,
                                        ALU.add, ALU.max).then_inc(hT_dve, 1)
            statistics(0)
            dve.wait_ge(params_ps, 2)
            nc.vector.tensor_copy(params[:, B:3 * B + E], bank[0][:, 0:2 * B + E]).then_inc(params_done, 1)
            deviation(0)
            for b in range(GB):
                normalize(b)
            statistics(1)

            def shared_hidden(i):
                (a, b), k = SEGMENTS[i // K2], i % K2
                dve.wait_ge(sg_done, i + 1)
                dve.wait_ge(su_ps, i + 1)
                nc.vector.tensor_tensor(hs[:, k, a * S:b * S], sg[:, i % 2, 0:(b - a) * S],
                                        bank[SH_BANKS[k][1]][:, 0:(b - a) * S], ALU.mult).then_inc(hs_done, 1)

            def residual(b):
                dve.wait_ge(sd_ps, b + 1)
                nc.vector.tensor_tensor(r_rows[:, b, :], bank[SH_Y[b % len(SH_Y)]][:, 0:H], x_tok[:, b, :], ALU.add
                                        ).then_inc(r_done, 1)

            def of(g, t):
                return t[:, g * GB:(g + 1) * GB]

            def numbers(g):
                return bank[NUM[g]][:, 0:GB * E].rearrange("p (b e) -> p b e", b=GB)

            def find_top(g):
                dve.wait_ge(logits_ps, g + 1)
                nc.vector.tensor_reduce(of(g, top), numbers(g), AX_X, ALU.max).then_inc(top_done, 1)

            def find_is_top(g):
                dve.wait_ge(top_done, g + 1)
                nc.vector.tensor_tensor(of(g, is_top), numbers(g), of(g, top).unsqueeze(2).to_broadcast([P, GB, E]),
                                        ALU.is_equal).then_inc(route[g], 1)

            def find_ranked(g):
                dve.wait_ge(route[g], 1)
                nc.vector.tensor_tensor(of(g, ranked), of(g, is_top), rev[:].unsqueeze(1).to_broadcast([P, GB, E]),
                                        ALU.mult).then_inc(route[g], 1)

            def find_first(g):
                dve.wait_ge(route[g], 2)
                nc.vector.tensor_reduce(of(g, first), of(g, ranked), AX_X, ALU.max).then_inc(route[g], 1)

            def find_hot(g):
                dve.wait_ge(route[g], 3)
                nc.vector.tensor_tensor(of(g, hot), of(g, ranked), of(g, first).unsqueeze(2).to_broadcast([P, GB, E]),
                                        ALU.is_equal).then_inc(hot_done, 1)

            def find_base(g):
                nc.vector.tensor_scalar(of(g, base), of(g, first), -float(P), float(P * E), ALU.mult, ALU.add
                                        ).then_inc(route[g], 1)

            def find_score(g):
                dve.wait_ge(tanh_done, g + 1)
                nc.vector.tensor_scalar(of(g, score), of(g, half_tanh), 0.5, 0.5, ALU.mult, ALU.add
                                        ).then_inc(score_done, 1)

            def find_over_n(g):
                dve.wait_ge(count_ps, g + 1)
                if g:
                    dve.wait_ge(over_n_done, g)
                nc.vector.tensor_scalar(over_k[:], thresholds[:], bank[4][0:E, COUNT:COUNT + 1], None, ALU.is_lt,
                                        ALU.add, accum_out=over_n[:, g:g + 1]).then_inc(over_n_done, 1)

            def find_place_hot(g):
                dve.wait_ge(pos_ps, g + 1)
                dve.wait_ge(hot_done, g + 1)
                nc.vector.tensor_tensor(of(g, place_hot), numbers(g), of(g, hot), ALU.mult).then_inc(pos_read, 1)

            def find_place(g):
                dve.wait_ge(pos_read, g + 1)
                nc.vector.tensor_reduce(of(g, place), of(g, place_hot), AX_X, ALU.add).then_inc(route[g], 1)

            def find_slot_fix(g):
                dve.wait_ge(route[g], 5)
                nc.vector.tensor_tensor(of(g, slot_fix), of(g, place), of(g, base), ALU.add).then_inc(route[g], 1)

            def find_shift_hot(g):
                dve.wait_ge(shift_ps, g + 1)
                at = AGAIN if g else FIRST
                nc.vector.tensor_tensor(of(g, shift_hot), of(g, hot),
                                        bank[4][:, at:at + E].unsqueeze(1).to_broadcast([P, GB, E]),
                                        ALU.mult).then_inc(route[g], 1)

            def find_shift(g, step):
                dve.wait_ge(route[g], step)
                nc.vector.tensor_reduce(of(g, shift), of(g, shift_hot), AX_X, ALU.add).then_inc(route[g], 1)

            def find_shifted(g, step, what):
                dve.wait_ge(route[g], step)
                nc.vector.scalar_tensor_tensor(out=of(g, shifted), in0=what, scalar=float(P), in1=of(g, shift),
                                               op0=ALU.is_ge, op1=ALU.mult).then_inc(route[g], 1)

            def find_slot(g, step, near):
                dve.wait_ge(route[g], step)
                nc.vector.tensor_tensor(of(g, slot), near, of(g, shifted), ALU.add).then_inc(slot_done, 1)

            dve.wait_ge(pool_const, 21)
            find_top(0)
            find_is_top(0)
            deviation(1)
            find_ranked(0)
            normalize(4)
            find_first(0)
            normalize(5)
            find_hot(0)
            find_base(0)
            normalize(6)
            find_score(0)
            find_over_n(0)
            find_place_hot(0)
            normalize(7)
            find_place(0)
            find_slot_fix(0)
            find_shift_hot(0)
            nc.vector.tensor_copy(table[:], bank[4][:, 0:AGAIN]).then_inc(table_done, 1)
            find_shift(0, 7)
            find_shifted(0, 8, of(0, place))
            find_slot(0, 9, of(0, slot_fix))
            find_top(1)
            find_is_top(1)
            find_ranked(1)
            find_first(1)
            find_hot(1)
            find_score(1)
            find_base(1)
            dve.wait_ge(hot_done, 2)
            dve.wait_ge(table_done, 1)
            nc.vector.tensor_tensor(pair_hot[:], of(1, hot).unsqueeze(2).to_broadcast([P, GB, 2, E]),
                                    table[:, FIRST:2 * E].rearrange("p (k e) -> p k e", k=2).unsqueeze(1)
                                    .to_broadcast([P, GB, 2, E]), ALU.mult).then_inc(route[1], 1)
            shared_hidden(0)
            find_over_n(1)
            find_place_hot(1)
            dve.wait_ge(route[1], 5)
            nc.vector.tensor_reduce(pair[:], pair_hot[:], AX_X, ALU.add).then_inc(route[1], 1)
            dve.wait_ge(pos_read, 2)
            nc.vector.tensor_reduce(of(1, place), of(1, place_hot), AX_X, ALU.add).then_inc(route[1], 1)
            dve.wait_ge(route[1], 7)
            nc.vector.tensor_tensor(of(1, slot_fix), of(1, place), of(1, base), ALU.add).then_inc(route[1], 1)
            nc.vector.scalar_tensor_tensor(out=of(1, shifted), in0=of(1, place), scalar=float(P), in1=pair[:, :, 0],
                                           op0=ALU.is_ge, op1=ALU.mult).then_inc(route[1], 1)
            find_shift_hot(1)
            nc.vector.tensor_tensor(beyond[:], of(1, place), pair[:, :, 1], ALU.subtract).then_inc(route[1], 1)
            dve.wait_ge(route[1], 9)
            nc.vector.tensor_tensor(slot_near[:], of(1, slot_fix), of(1, shifted), ALU.add).then_inc(route[1], 1)
            find_shift(1, 10)
            find_shifted(1, 13, beyond[:])
            find_slot(1, 14, slot_near[:])
            shared_hidden(1)
            nc.vector.tensor_tensor(starts_kept[:], table[0:1, FIRST:E], table[0:1, KEPT:KEPT + E], ALU.add
                                    ).then_inc(route[1], 1)
            nc.vector.tensor_tensor(past[:, :, 0, :], table[0:1, 1:E].unsqueeze(1).to_broadcast([1, OVER, E - 1]),
                                    bounds[:], ALU.is_le).then_inc(route[1], 1)
            nc.vector.tensor_scalar(own[:], steps[:], table[0:1, USED:USED + 1], float(E - 1), ALU.is_ge, ALU.mult
                                    ).then_inc(route[1], 1)
            dve.wait_ge(route[1], 17)
            nc.vector.tensor_tensor(starts[:], starts_kept[:], bank[4][0:1, AGAIN:ALL], ALU.add).then_inc(route[1], 1)
            dve.wait_ge(route[1], 18)
            nc.vector.tensor_tensor(past[:, :, 1, :], starts[:, 1:E].unsqueeze(1).to_broadcast([1, OVER, E - 1]),
                                    bounds[:], ALU.is_le).then_inc(route[1], 1)
            dve.wait_ge(route[1], 19)
            nc.vector.tensor_reduce(past_sum[:], past[:].rearrange("p j k e -> p j (k e)"), AX_X, ALU.add
                                    ).then_inc(route[1], 1)
            dve.wait_ge(route[1], 20)
            nc.vector.tensor_tensor(over_ex_f[:], past_sum[:], own[:], ALU.subtract).then_inc(route[1], 1)
            nc.vector.tensor_copy(over_size[:], bank[4][0:1, ALL:ALL + 1]).then_inc(over_ex_done, 1)
            dve.wait_ge(route[1], 21)
            nc.vector.tensor_copy(over_ex[:], over_ex_f[:]).then_inc(over_ex_done, 1)
            shared_hidden(2)
            residual(0)
            shared_hidden(3)
            for b in range(1, B):
                residual(b)

            def expert_tiles(run):
                def gated(i):
                    dve.wait_ge(run.eg_done, i + 1)
                    if i >= 3:
                        dve.wait_ge(run.ehT_ps if i - 3 < run.over else run.y_ps, i - 2)
                    nc.vector.tensor_tensor(eh[:, i % 3, :], eg[:, i % 2, :], bank[EX_GU[i % 2]][:, FF:2 * FF],
                                            ALU.mult).then_inc(run.eh_done, 1)

                def y_copy(i):
                    dve.wait_ge(run.y_ps, i + 1)
                    nc.vector.tensor_copy(y[:, run.tiles[i], :], bank[EX_Y[i % 2]][:, 0:H]).then_inc(run.y_copied, 1)

                def add_r(i):
                    tile = run.tiles[i]
                    dve.wait_ge(run.y_copied, i + 1)
                    dve.wait_ge(slot_r_in[piece_of(tile)], 16)
                    nc.vector.tensor_tensor(y[:, tile, :], y[:, tile, :], slot_r[:, tile, :], ALU.add
                                            ).then_inc(run.y_done, 1)

                def y_finish(i):
                    tile = run.tiles[i]
                    dve.wait_ge(run.y_ps, i + 1)
                    dve.wait_ge(slot_r_in[piece_of(tile)], 16)
                    nc.vector.tensor_tensor(y[:, tile, :], bank[EX_Y[i % 2]][:, 0:H], slot_r[:, tile, :], ALU.add
                                            ).then_inc(run.y_done, 1)

                for i in range(run.n + 2):
                    if i >= 2:
                        (y_copy if i - 2 < run.copied else y_finish)(i - 2)
                    if i == run.lag:
                        add_r(0)
                    if i < run.n:
                        gated(i)
                    for k in range(2 * (i - run.lag), min(2 * (i - run.lag) + 2, run.copied)):
                        if k >= 1:
                            add_r(k)

            with nc.vector.If(rare_in_use(nc.vector)):
                expert_tiles(rare)
            expert_tiles(main)


_INS = ["x", "itok_B_0_8", "L0_cond_W1", "L0_cond_b1", "L0_cond_W2", "L0_cond_b2", "L0_cond_gamma", "L0_cond_beta",
        "L0_ffn_router_w", "L0_ffn_expert_gate", "L0_ffn_expert_up", "L0_ffn_expert_down",
        "L0_ffn_shared_gate", "L0_ffn_shared_up", "L0_ffn_shared_down"]


def kernel(**inputs):
    import numpy as _np
    import concourse.bacc as _bacc
    from concourse import mybir as _mybir
    from concourse.bass_utils import run_bass_kernel_spmd as _run

    nc = _bacc.Bacc("TRN2", target_bir_lowering=False, num_devices=1)
    arrays, args = {}, []
    for name in _INS:
        a = _np.ascontiguousarray(inputs[name])
        arrays[f"in_{name}_dram"] = a
        args.append(nc.dram_tensor(f"in_{name}_dram", a.shape, _mybir.dt.from_np(a.dtype), kind="ExternalInput").ap())
    out = nc.dram_tensor("out_dram", inputs["x"].shape, _mybir.dt.float32, kind="ExternalOutput").ap()
    adaln_moe_kernel(nc, *args, out)
    r = _run(nc, [arrays], core_ids=[0])
    return r.results[0]["out_dram"]
```
